# Optimizing a Trainium2 kernel written in Bass

```python
import numpy as np
import jax
import jax.numpy as jnp

def _softmax(x, axis=-1):
    return jax.nn.softmax(x, axis=axis)

def _gelu(x):
    return jax.nn.gelu(x, approximate=True)

def _silu(x):
    return jax.nn.silu(x)

def _sigmoid(x):
    return jax.nn.sigmoid(x)

def _layernorm(x, axis=-1, eps=1e-05):
    m = jnp.mean(x, axis=axis, keepdims=True)
    v = jnp.var(x, axis=axis, keepdims=True)
    return (x - m) / jnp.sqrt(v + eps)

def _scatter_add(tgt, idx, src, axis=0):
    return tgt.at[idx].add(src)

def _segment_sum(src, seg, n):
    return jax.ops.segment_sum(src, seg, n)
kernel_name = 'mk_hybrid_d1_jaxref_r8_c09603'

def setup_inputs(seed: int=0):
    np.random.seed(seed)
    _w = jnp.asarray

    def _L0_attn_a_setup():
        import jax, jax.numpy as jnp
        import numpy as np
        HIDDEN = 128
        EXPAND = 2
        D_REC = HIDDEN * EXPAND
        INTER = 512
        B, T = (4, 512)

        def _rmsnorm(x, w, eps=1e-06):
            var = jnp.mean(x * x, axis=-1, keepdims=True)
            return x * jax.lax.rsqrt(var + eps) * w

        def _hawk_scan(x_in, a):
            xs = jnp.moveaxis(x_in, 1, 0)
            As = jnp.moveaxis(a, 1, 0)

            def step(state, inp):
                a_t, x_t = inp
                new = a_t * state + jnp.sqrt(1.0 - a_t * a_t + 1e-08) * x_t
                return (new, new)
            init = jnp.zeros(x_in.shape[::2], dtype=x_in.dtype)
            _, ys = jax.lax.scan(step, init, (As, xs))
            return jnp.moveaxis(ys, 0, 1)
        key = jax.random.key(seed)
        ks = jax.random.split(key, 11)
        s = lambda fan: 1.0 / np.sqrt(fan)
        return {'x': jax.random.normal(ks[0], (B, T, HIDDEN), dtype=jnp.float32), 'ln1_w': jnp.ones((HIDDEN,), dtype=jnp.float32), 'ln2_w': jnp.ones((HIDDEN,), dtype=jnp.float32), 'w_in': jax.random.normal(ks[1], (D_REC, HIDDEN), dtype=jnp.float32) * s(HIDDEN), 'w_gate': jax.random.normal(ks[2], (D_REC, HIDDEN), dtype=jnp.float32) * s(HIDDEN), 'a_param': jax.random.normal(ks[3], (D_REC,), dtype=jnp.float32) * 0.1, 'w_a': jax.random.normal(ks[4], (D_REC, D_REC), dtype=jnp.float32) * s(D_REC), 'w_out': jax.random.normal(ks[5], (HIDDEN, D_REC), dtype=jnp.float32) * s(D_REC), 'w_mlp_gate': jax.random.normal(ks[6], (INTER, HIDDEN), dtype=jnp.float32) * s(HIDDEN), 'w_mlp_up': jax.random.normal(ks[7], (INTER, HIDDEN), dtype=jnp.float32) * s(HIDDEN), 'w_mlp_down': jax.random.normal(ks[8], (HIDDEN, INTER), dtype=jnp.float32) * s(INTER)}
    _L0_attn_a_in = _L0_attn_a_setup()

    def _L0_attn_b_setup():
        import jax, jax.numpy as jnp
        import numpy as np
        B, S, D, H = (2, 256, 128, 16)
        HD = D // H
        EPS = 1e-05
        key = jax.random.key(seed)
        kx, kq, kk, kv, kb = jax.random.split(key, 5)
        sc = 0.02
        return {'x': jax.random.normal(kx, (B, S, D), dtype=jnp.float32), 'Wq': jax.random.normal(kq, (D, D), dtype=jnp.float32) * sc, 'Wk': jax.random.normal(kk, (D, D), dtype=jnp.float32) * sc, 'Wv': jax.random.normal(kv, (D, D), dtype=jnp.float32) * sc, 'rel_bias_table': jax.random.normal(kb, (2 * S - 1, H), dtype=jnp.float32) * sc, 'ln_gamma': jnp.ones((D,), dtype=jnp.float32), 'ln_beta': jnp.zeros((D,), dtype=jnp.float32)}
    _L0_attn_b_in = _L0_attn_b_setup()

    def _L0_ffn_setup():
        import jax, jax.numpy as jnp
        import numpy as np
        B, S, D_MODEL, D_FF, E, R, TOP_K = (4, 256, 128, 512, 8, 16, 2)
        key = jax.random.key(seed)
        ks = jax.random.split(key, 9)
        sd = 1.0 / np.sqrt(D_MODEL)
        return {'hidden_states': jax.random.normal(ks[0], (B, S, D_MODEL), jnp.float32), 'wi': jax.random.normal(ks[1], (D_FF, D_MODEL), jnp.float32) * sd, 'bi': jax.random.normal(ks[2], (D_FF,), jnp.float32) * 0.01, 'wo': jax.random.normal(ks[3], (D_MODEL, D_FF), jnp.float32) * (1.0 / np.sqrt(D_FF)), 'bo': jax.random.normal(ks[4], (D_MODEL,), jnp.float32) * 0.01, 'lora_A': jax.random.normal(ks[5], (E, R, D_MODEL), jnp.float32) * sd, 'lora_B': jax.random.normal(ks[6], (E, D_FF, R), jnp.float32) * 0.02, 'gate_w': jax.random.normal(ks[7], (E, D_MODEL), jnp.float32) * sd, 'gate_b': jax.random.normal(ks[8], (E,), jnp.float32) * 0.01}
    _L0_ffn_in = _L0_ffn_setup()
    _d = {'L0_attn_a_x': _L0_attn_a_in['x'], 'L0_attn_a_ln1_w': _L0_attn_a_in['ln1_w'], 'L0_attn_a_ln2_w': _L0_attn_a_in['ln2_w'], 'L0_attn_a_w_in': _L0_attn_a_in['w_in'], 'L0_attn_a_w_gate': _L0_attn_a_in['w_gate'], 'L0_attn_a_a_param': _L0_attn_a_in['a_param'], 'L0_attn_a_w_a': _L0_attn_a_in['w_a'], 'L0_attn_a_w_out': _L0_attn_a_in['w_out'], 'L0_attn_a_w_mlp_gate': _L0_attn_a_in['w_mlp_gate'], 'L0_attn_a_w_mlp_up': _L0_attn_a_in['w_mlp_up'], 'L0_attn_a_w_mlp_down': _L0_attn_a_in['w_mlp_down'], 'L0_attn_b_Wq': _L0_attn_b_in['Wq'], 'L0_attn_b_Wk': _L0_attn_b_in['Wk'], 'L0_attn_b_Wv': _L0_attn_b_in['Wv'], 'L0_attn_b_rel_bias_table': _L0_attn_b_in['rel_bias_table'], 'L0_attn_b_ln_gamma': _L0_attn_b_in['ln_gamma'], 'L0_attn_b_ln_beta': _L0_attn_b_in['ln_beta'], 'L0_ffn_wi': _L0_ffn_in['wi'], 'L0_ffn_bi': _L0_ffn_in['bi'], 'L0_ffn_wo': _L0_ffn_in['wo'], 'L0_ffn_bo': _L0_ffn_in['bo'], 'L0_ffn_lora_A': _L0_ffn_in['lora_A'], 'L0_ffn_lora_B': _L0_ffn_in['lora_B'], 'L0_ffn_gate_w': _L0_ffn_in['gate_w'], 'L0_ffn_gate_b': _L0_ffn_in['gate_b']}
    _x0 = _d['L0_attn_a_x']
    _d['L0_attn_a_x'] = jax.random.normal(jax.random.fold_in(jax.random.key(seed), 1), (2, 1024, 128), dtype=_x0.dtype)
    del _x0
    return _d

def reference(L0_attn_a_x, L0_attn_a_ln1_w, L0_attn_a_ln2_w, L0_attn_a_w_in, L0_attn_a_w_gate, L0_attn_a_a_param, L0_attn_a_w_a, L0_attn_a_w_out, L0_attn_a_w_mlp_gate, L0_attn_a_w_mlp_up, L0_attn_a_w_mlp_down, L0_attn_b_Wq, L0_attn_b_Wk, L0_attn_b_Wv, L0_attn_b_rel_bias_table, L0_attn_b_ln_gamma, L0_attn_b_ln_beta, L0_ffn_wi, L0_ffn_bi, L0_ffn_wo, L0_ffn_bo, L0_ffn_lora_A, L0_ffn_lora_B, L0_ffn_gate_w, L0_ffn_gate_b):

    def _L0_attn_a_ref(x, ln1_w, ln2_w, w_in, w_gate, a_param, w_a, w_out, w_mlp_gate, w_mlp_up, w_mlp_down):
        import jax, jax.numpy as jnp
        import numpy as np
        HIDDEN = 128
        EXPAND = 2
        D_REC = HIDDEN * EXPAND
        INTER = 512
        B, T = (4, 512)

        def _rmsnorm(x, w, eps=1e-06):
            var = jnp.mean(x * x, axis=-1, keepdims=True)
            return x * jax.lax.rsqrt(var + eps) * w

        def _hawk_scan(x_in, a):
            xs = jnp.moveaxis(x_in, 1, 0)
            As = jnp.moveaxis(a, 1, 0)

            def step(state, inp):
                a_t, x_t = inp
                new = a_t * state + jnp.sqrt(1.0 - a_t * a_t + 1e-08) * x_t
                return (new, new)
            init = jnp.zeros(x_in.shape[::2], dtype=x_in.dtype)
            _, ys = jax.lax.scan(step, init, (As, xs))
            return jnp.moveaxis(ys, 0, 1)
        h = _rmsnorm(x, ln1_w)
        x_in = h @ w_in.T
        gate = jax.nn.sigmoid(h @ w_gate.T)
        a = jax.nn.sigmoid(a_param + x_in @ w_a.T)
        y = gate * _hawk_scan(x_in, a)
        x = x + y @ w_out.T
        h2 = _rmsnorm(x, ln2_w)
        mlp = jax.nn.silu(h2 @ w_mlp_gate.T) * (h2 @ w_mlp_up.T) @ w_mlp_down.T
        return x + mlp

    def _L0_attn_b_ref(x, Wq, Wk, Wv, rel_bias_table, ln_gamma, ln_beta):
        import jax, jax.numpy as jnp
        import numpy as np
        B, S, D, H = (2, 256, 128, 16)
        HD = D // H
        EPS = 1e-05
        bs, seq_len, d_model = x.shape
        scale = d_model ** (-0.5)
        q = jnp.einsum('bsd,ed->bse', x, Wq).reshape(bs, seq_len, H, HD).transpose(0, 2, 1, 3)
        k = jnp.einsum('bsd,ed->bse', x, Wk).reshape(bs, seq_len, H, HD).transpose(0, 2, 1, 3)
        v = jnp.einsum('bsd,ed->bse', x, Wv).reshape(bs, seq_len, H, HD).transpose(0, 2, 1, 3)
        attn = jax.nn.softmax(jnp.einsum('bhqd,bhkd->bhqk', q, k) * scale, axis=-1)
        idx = jnp.arange(seq_len)[:, None] - jnp.arange(seq_len)[None, :] + (seq_len - 1)
        rel_bias = rel_bias_table[idx]
        rel_bias = rel_bias.transpose(2, 0, 1)[None]
        attn = attn + rel_bias
        out = jnp.einsum('bhqk,bhkd->bhqd', attn, v)
        out = out.transpose(0, 2, 1, 3).reshape(bs, seq_len, d_model)
        mu = jnp.mean(out, axis=-1, keepdims=True)
        var = jnp.var(out, axis=-1, keepdims=True)
        out = (out - mu) * jax.lax.rsqrt(var + EPS)
        return out * ln_gamma + ln_beta

    def _L0_ffn_ref(hidden_states, wi, bi, wo, bo, lora_A, lora_B, gate_w, gate_b):
        import jax, jax.numpy as jnp
        import numpy as np
        B, S, D_MODEL, D_FF, E, R, TOP_K = (4, 256, 128, 512, 8, 16, 2)
        logits = jnp.einsum('bsd,ed->bse', hidden_states, gate_w) + gate_b
        scores = jax.nn.softmax(logits, axis=-1)
        top_v, top_i = jax.lax.top_k(scores, TOP_K)
        val_sum = top_v.sum(axis=-1)
        out = jnp.zeros_like(hidden_states)
        for e in range(E):
            count = (top_i == e).sum(axis=-1).astype(hidden_states.dtype)
            gate = count * val_sum
            inter = jnp.einsum('bsd,fd->bsf', hidden_states, wi) + bi + jnp.einsum('bsr,fr->bsf', jnp.einsum('bsd,rd->bsr', hidden_states, lora_A[e]), lora_B[e])
            h = jax.nn.relu(inter)
            expert_out = jnp.einsum('bsf,df->bsd', h, wo) + bo
            out = out + gate[..., None] * expert_out
        return out
    x = L0_attn_a_x
    x = x + _L0_attn_a_ref(_layernorm(x, axis=-1), L0_attn_a_ln1_w, L0_attn_a_ln2_w, L0_attn_a_w_in, L0_attn_a_w_gate, L0_attn_a_a_param, L0_attn_a_w_a, L0_attn_a_w_out, L0_attn_a_w_mlp_gate, L0_attn_a_w_mlp_up, L0_attn_a_w_mlp_down)
    x = x + _L0_ffn_ref(_layernorm(x, axis=-1), L0_ffn_wi, L0_ffn_bi, L0_ffn_wo, L0_ffn_bo, L0_ffn_lora_A, L0_ffn_lora_B, L0_ffn_gate_w, L0_ffn_gate_b)
    x = x + _L0_attn_b_ref(_layernorm(x, axis=-1), L0_attn_b_Wq, L0_attn_b_Wk, L0_attn_b_Wv, L0_attn_b_rel_bias_table, L0_attn_b_ln_gamma, L0_attn_b_ln_beta)
    x = x + _L0_ffn_ref(_layernorm(x, axis=-1), L0_ffn_wi, L0_ffn_bi, L0_ffn_wo, L0_ffn_bo, L0_ffn_lora_A, L0_ffn_lora_B, L0_ffn_gate_w, L0_ffn_gate_b)
    return x

_drawn_inputs = setup_inputs


def setup_inputs(seed=0):
    import zlib

    import numpy as np

    out = dict(_drawn_inputs(seed))
    spreads = {'L0_attn_a_ln1_w': (1.0, 0.2),
     'L0_attn_a_ln2_w': (1.0, 0.2),
     'L0_attn_b_ln_gamma': (1.0, 0.2),
     'L0_attn_b_ln_beta': (0.0, 0.1)}
    factors = {'L0_attn_a_a_param': 6.435,
     'L0_attn_b_Wq': 61.497,
     'L0_attn_b_Wk': 60.39,
     'L0_ffn_bi': 8.0,
     'L0_ffn_bo': 4.726,
     'L0_ffn_gate_b': 8.0}
    for name, (base, spread) in spreads.items():
        noise = np.random.default_rng([zlib.crc32(name.encode()), seed]).standard_normal(out[name].shape)
        drawn = base * np.exp(spread * noise) if base else spread * noise
        out[name] = jnp.asarray(drawn.astype(out[name].dtype))
    for name, factor in factors.items():
        out[name] = (out[name] * factor).astype(out[name].dtype)
    return out
```

```python
import numpy as np
import concourse.bass as bass
from concourse import mybir
from contextlib import ExitStack

FP32 = mybir.dt.float32
BF16 = mybir.dt.bfloat16
ALU = mybir.AluOpType
ACT = mybir.ActivationFunctionType
AXX = mybir.AxisListType.X

P = 128
NB = 2
S = 1024
NT = S // P
HALF = S // 2
TH = NT // 2
REC = 2
FC = 4
NE, RANK = 8, 16
UW = P + NE
NH, HD = 16, 8
GH = 4
NG = NH // GH
NPART = 3
STACK = NPART * NPART * HD
DEPTH = STACK + NPART
NBUF = 3
VW = 32
BIASW = 512
LAST = 510
LN_EPS, RMS_EPS = 1e-5, 1e-6
ONE_PAIR = float(np.array([0x3F803F80], np.uint32).view(np.float32)[0])
ARENA = 22 * S // 2
SCALE = float(P) ** -0.5
UNDERFLOW = -87.336544
N_CONSTS = 6 + NE

N_REC, N_MLP, N_FFN0, N_ATTN, N_OUT, N_FFN1 = range(6)
TRANSPOSED = {N_REC: 0, N_MLP: 1, N_FFN0: 2, N_ATTN: 3, N_FFN1: 4}


def ffn_jobs(f):
    jobs = [(f"T{f}.{h}", h, "act") for h in range(2)]
    jobs += [(f"U{f}.{j}", 2 + j, "dve") for j in range(4)]
    for h in range(2):
        jobs += [(f"X{f}.{h}.{k}", k, "act") for k in range(2)]
        for c in range(FC):
            jobs.append((f"HA{f}.{h}.{c}", (6, 7, 4, 5)[c], "act"))
        for c in range(FC):
            jobs.append((f"HB{f}.{h}.{c}", (6, 7, 4, 5)[c], "dve"))
    for h in range(2):
        jobs.append((f"O{f}.{h}", 2 + h, "act"))
    for h in range(2):
        jobs.append((f"R{f}.{h}", h, "dve"))
    return jobs


def all_jobs():
    jobs = [(f"Trec.{h}", h, "act") for h in range(2)]
    jobs += [(f"XI.{h}.{c}", 2 + 2 * h + c, "act") for h in range(2) for c in range(REC)]
    jobs += [(f"G.{h}.{c}", (6, 7, 0, 1)[2 * h + c], "act") for h in range(2) for c in range(REC)]
    jobs += [(f"A.{h}.{c}", 2 + 2 * h + c, "act") for c in range(REC) for h in range(2)]
    jobs += [(f"WO.{h}", 6 + h, "act") for h in range(2)]
    jobs += [(f"Rrec.{h}", h, "dve") for h in range(2)]
    jobs += [(f"Tmlp.{h}", 2 + h, "act") for h in range(2)]
    for h in range(2):
        for c in range(FC):
            jobs.append((f"MG.{h}.{c}", 4 + (c % 2), "dve"))
            jobs.append((f"MU.{h}.{c}", 6 + (c % 2), "dve"))
        jobs.append((f"MD.{h}", h, "act"))
    jobs += [(f"Rmlp.{h}", 2 + h, "dve") for h in range(2)]
    jobs += ffn_jobs(0)
    jobs += [(f"Tatt.{h}", h, "act") for h in range(2)]
    jobs += [(f"QK.{w}.{h}", 2 + 2 * w + h, "dve") for w in range(2) for h in range(2)]
    jobs += [(f"V.{h}", 6 + h, "dve") for h in range(2)]
    jobs.append(("CS", 0, "dve"))
    jobs += ffn_jobs(1)
    return jobs


JOBS = all_jobs()
NJOBS = len(JOBS)
INDEX = {name: i for i, (name, _, _) in enumerate(JOBS)}
BANK = {name: bank for name, bank, _ in JOBS}
N_EMPTIED = {e: sum(c == e for _, _, c in JOBS) for e in ("act", "dve")}
EMPTYING = {name: (c, sum(x[2] == c for x in JOBS[: i + 1])) for i, (name, _, c) in enumerate(JOBS)}
BEFORE = {name: ([None] + [n for n, k, _ in JOBS[:i] if k == bank])[-1] for i, (name, bank, _) in enumerate(JOBS)}

STEPS = NT * 2
MAXES = GH * NT
FAST = 13


def ring_items(g, s):
    items = []
    if s == 2 and g > 0:
        items += [("otr", g - 1), ("btr", g - 1)]
    if g + 1 < NG:
        items += [("max", g + 1, n) for n in range(MAXES * s // FAST, MAXES * (s + 1) // FAST) if n < MAXES]
    if s == FAST and g + 1 < NG:
        items.append(("mtr", g + 1))
    if s == FAST + 1:
        items.append(("bias", g))
    return items


RING = [("max", 0, n) for n in range(MAXES)] + [("mtr", 0)]
for _g in range(NG):
    for _s in range(STEPS):
        RING += ring_items(_g, _s)
RING += [("otr", NG - 1), ("btr", NG - 1)]
SLOT = {item: i for i, item in enumerate(RING)}
NRING = len(RING)


def build(nc, x_in, out, w, tab):
    ctx = ExitStack()
    with ctx:
        def sb(name, shape, dt=FP32):
            return ctx.enter_context(nc.sbuf_tensor(name, shape, dt))

        def sem(name):
            return ctx.enter_context(nc.semaphore(name))

        w_inT = sb("w_inT", [P, REC * P])
        w_gateT = sb("w_gateT", [P, REC * P])
        w_aT = sb("w_aT", [P, REC, REC * P])
        w_outT = sb("w_outT", [P, REC, P])
        mgT = sb("mgT", [P, FC * P])
        muT = sb("muT", [P, FC * P])
        mdT = sb("mdT", [P, FC, P])
        a_param = sb("a_param", [P, REC])
        ln1_w = sb("ln1_w", [P, 1])
        ln2_w = sb("ln2_w", [P, 1])
        wiT = sb("wiT", [P, FC * P])
        bi = sb("bi", [P, FC])
        woT = sb("woT", [P, FC, P])
        bo = sb("bo", [P, 1])
        bo2 = sb("bo2", [P, 1])
        agT = sb("agT", [P, UW])
        bT = sb("bT", [P, FC * P])
        gate_b = sb("gate_b", [P, NE])
        wqkvT = sb("wqkvT", [P, 3, P])
        gamma = sb("gamma", [P, P])
        beta = sb("beta", [P, P])
        t_last = sb("t_last", [P, NH])
        master = sb("master", [P, NH, BIASW])
        varying = sb("varying", [P, GH, BIASW])
        ident = sb("ident", [P, P])
        ones = sb("ones", [P, P])
        rank_of = sb("rank_of", [P, NE])
        one_pair = sb("one_pair", [P, 1])
        neghalf = sb("neghalf", [P, 2 * TH])
        tiny = sb("tiny", [P, 1])

        x0 = sb("x0", [P, NT, P])
        z = sb("z", [P, NT, P])
        x1 = sb("x1", [P, NT, P])
        x = sb("x", [P, NT, P])
        nt = sb("nt", [P, NT, P])
        o_tok = sb("o_tok", [P, NT, P])
        stats = sb("stats", [P, NT, 6])
        mv = sb("mv", [P, NT, 2])
        veps = sb("veps", [P, 2, 2 * TH])
        rstd = sb("rstd", [P, 2, 2 * TH])
        msq = sb("msq", [P, NT])
        mr = sb("mr", [P, NT])
        arena = sb("arena", [P, ARENA])

        def carve(*shapes):
            at_, tiles_ = 0, []
            for shape in shapes:
                size = 1
                for n in shape:
                    size *= n
                assert at_ + size <= ARENA
                flat = arena[:, at_:at_ + size]
                axes = " ".join(f"a{i}" for i in range(len(shape)))
                tiles_.append(flat.rearrange(f"p ({axes}) -> p {axes}", **{f"a{i}": n for i, n in enumerate(shape)}) if len(shape) > 1 else flat)
                at_ += size
            return tiles_

        xinT, gT, aT, sT, yT = carve(*[[REC, S]] * 5)
        sg, sgu, m_T = carve([2, HALF], [2, HALF], [FC, S])
        h0, h1, hs, um, umT = carve([FC, HALF], [2, HALF], [FC, S], [2, NT, P], [2, S])
        probs, pvT, biasT, qk_rest, qk_words = carve([2, GH, HALF], [S], [BIASW], [2, S], [2 * NPART * S // 2])
        qk_part = qk_words.bitcast(BF16).rearrange("p (w n t) -> p w n t", w=2, n=NPART)
        hT = sb("hT", [P, S])
        oT = sb("oT", [P, S])
        lg = sb("lg", [P, NT, NE])
        ls = sb("ls", [P, NT, NE])
        ex = sb("ex", [P, NT, NE])
        key = sb("key", [P, NT, NE])
        pick0 = sb("pick0", [P, NT, NE])
        pick1 = sb("pick1", [P, NT, NE])
        pickd = sb("pickd", [P, NT, NE])
        ls2 = sb("ls2", [P, NT, NE])
        zero_t = sb("zero_t", [P, NT])
        m1 = sb("m1", [P, NT])
        m2 = sb("m2", [P, NT])
        k1 = sb("k1", [P, NT])
        k2 = sb("k2", [P, NT])
        esum = sb("esum", [P, NT])
        ersum = sb("ersum", [P, NT])
        e2 = sb("e2", [P, NT])
        val = sb("val", [P, NT])
        qs = sb("qs", [P, NBUF, GH, S], BF16)
        ks = sb("ks", [P, NBUF, GH, S], BF16)
        vp = sb("vp", [P, NT, NH, VW])
        cs = sb("cs", [P, P])
        negmax = sb("negmax", [P, 2, GH * NT])
        nm_rest = sb("nm_rest", [GH * NT, P])
        nm_part = sb("nm_part", [GH * NT, 2, NPART, P], BF16)
        rl = sb("rl", [P, NT, GH])

        scratch = nc.dram_tensor("qk_scratch", (2, NPART, P, S), BF16, kind="Internal").ap()
        banks = ctx.enter_context(nc.psum_tensor("banks", [P, 8, HALF], FP32))

        def ring(item):
            return banks[:, 2 * (SLOT[item] % 2):2 * (SLOT[item] % 2) + 2, :]

        def score_bank(n):
            return banks[:, 4 + n % 2, :]

        def pv_bank(q):
            return banks[:, 6 + q, :]

        w_rec, w_mlp, w_ffn, w_att, w_bias = (sem(n) for n in ("w_rec", "w_mlp", "w_ffn", "w_att", "w_bias"))
        k_ones = sem("k_ones")
        zeroed, consts, bo2_ready = sem("zeroed"), sem("consts"), sem("bo2_ready")
        x_loaded, x0_used, stored = sem("x_loaded"), sem("x0_used"), sem("stored")
        z_ready, varying_ready = sem("z_ready"), sem("varying_ready")
        filled, act_emptied, dve_emptied = sem("filled"), sem("act_emptied"), sem("dve_emptied")
        stats_ready, rstd_ready, norm_ready = sem("stats_ready"), sem("rstd_ready"), sem("norm_ready")
        one_minus_sq, root_ready, y_ready = sem("one_minus_sq"), sem("root_ready"), sem("y_ready")
        gate_sig = sem("gate_sig")
        logits_ready, exps_ready, second_ready, exp2_ready = (sem(n) for n in ("logits_ready", "exps_ready", "second_ready", "exp2_ready"))
        u_masked, h_ready = sem("u_masked"), sem("h_ready")
        qk_high, qk_mid, qk_low, qk_stored = sem("qk_high"), sem("qk_mid"), sem("qk_low"), sem("qk_stored")
        qk_loaded = [sem(f"qk_loaded{i}") for i in range(NBUF)]
        ring_filled, ring_emptied = sem("ring_filled"), sem("ring_emptied")
        negmax_split = sem("negmax_split")
        negmax_loaded = [sem(f"negmax_loaded{i}") for i in range(NG)]
        scores_filled, exp_done, pv_done, pv_out = sem("scores_filled"), sem("exp_done"), sem("pv_done"), sem("pv_out")
        bias_out = sem("bias_out")
        n_exp = NG * STEPS * GH
        PER_BATCH = {
            filled: NJOBS, act_emptied: N_EMPTIED["act"], dve_emptied: N_EMPTIED["dve"],
            stats_ready: 12, rstd_ready: 12, norm_ready: 10, one_minus_sq: REC, root_ready: REC, y_ready: REC,
            gate_sig: 2 * FC, logits_ready: 2, exps_ready: 2, second_ready: 2, exp2_ready: 2,
            u_masked: 8, h_ready: 4 * FC, qk_high: 4, qk_mid: 4, qk_low: 4,
            ring_filled: NRING, ring_emptied: NRING, negmax_split: NG,
            scores_filled: n_exp, exp_done: n_exp, pv_done: NG * STEPS, pv_out: 2 * NG, bias_out: NG,
            x0_used: 1, stored: 32, z_ready: 1, varying_ready: NG,
        }

        CREDIT = {act_emptied: 1, dve_emptied: 1, x0_used: 1, stored: 16}

        def at(b, s, k):
            return b * PER_BATCH[s] + k + CREDIT.get(s, 0)

        def emptied(b, name):
            engine, k = EMPTYING[name]
            s = act_emptied if engine == "act" else dve_emptied
            return s, at(b, s, k)

        block = ctx.enter_context(nc.Block())

        @block.sync
        def _(sp):
            for dst, src in ((ln1_w[:], w["ln1_w"]), (w_inT[:], w["w_inT"]), (w_gateT[:], w["w_gateT"]),
                             (w_aT[:], w["w_aT"].rearrange("(k p) n -> p k n", p=P)), (a_param[:], w["a_param"]),
                             (w_outT[:], w["w_outT"].rearrange("(k p) n -> p k n", p=P))):
                sp.dma_start(dst, src).then_inc(w_rec, 16)
            for dst, src in ((ln2_w[:], w["ln2_w"]), (mgT[:], w["mgT"]), (muT[:], w["muT"]),
                             (mdT[:], w["mdT"].rearrange("(k p) n -> p k n", p=P))):
                sp.dma_start(dst, src).then_inc(w_mlp, 16)
            for dst, src in ((wiT[:], w["wiT"]), (bi[:], w["bi"]), (woT[:], w["woT"].rearrange("(k p) n -> p k n", p=P)),
                             (bo[:], w["bo"]), (agT[:], w["agT"]), (bT[:], w["bT"]),
                             (gate_b[:], w["gate_b"].broadcast_to([P, NE]))):
                sp.dma_start(dst, src).then_inc(w_ffn, 16)
            for dst, src in ((wqkvT[:], w["wqkvT"].rearrange("(k p) n -> p k n", p=P)),
                             (gamma[:], w["gamma"].broadcast_to([P, P])), (beta[:], w["beta"].broadcast_to([P, P]))):
                sp.dma_start(dst, src).then_inc(w_att, 16)
            sp.dma_start(master[:], bass.AP(tensor=tab.tensor, offset=0, ap=[[1, P], [tab.shape[1], NH], [1, BIASW]])).then_inc(w_bias, 16)
            sp.dma_start(t_last[:], w["t_last"].broadcast_to([P, NH])).then_inc(w_bias, 16)

            def load_products(b, g):
                heads = slice(g * GH * HD, (g + 1) * GH * HD)
                for i in range(NPART):
                    for j in range(NPART):
                        rows = slice((i * NPART + j) * HD, (i * NPART + j + 1) * HD)
                        sp.dma_start(qs[rows, g % NBUF, :, :], scratch[0, i, heads, :].rearrange("(h d) t -> d h t", d=HD)).then_inc(qk_loaded[g % NBUF], 16)
                        sp.dma_start(ks[rows, g % NBUF, :, :], scratch[1, j, heads, :].rearrange("(h d) t -> d h t", d=HD)).then_inc(qk_loaded[g % NBUF], 16)

            def load_negmax(b, g):
                sp.wait_ge(negmax_split, at(b, negmax_split, g + 1))
                for i in range(NPART):
                    sp.dma_start(qs[STACK + i:STACK + i + 1, g % NBUF, :, :].rearrange("o h (t q) -> o (h t) q", q=P),
                                 nm_part[:, g % 2, i, :]).then_inc(negmax_loaded[g], 16)

            sp.wait_ge(k_ones, 1)
            sp.nop().then_inc(stored, CREDIT[stored])
            with sp.Fori(0, NB) as b:
                for k in range(4):
                    which, h = k // 2, k % 2
                    sp.wait_ge(qk_low, at(b, qk_low, k + 1))
                    sp.dma_start(scratch[which, :, :, h * HALF:(h + 1) * HALF].rearrange("n p t -> p n t"),
                                 qk_part[:, which, :, h * HALF:(h + 1) * HALF]).then_inc(qk_stored, 16)
                sp.wait_ge(qk_stored, b * 64 + 64)
                for g in range(NBUF):
                    load_products(b, g)
                for g in range(NG):
                    load_negmax(b, g)
                    if g >= 1 and g - 1 + NBUF < NG:
                        sp.wait_ge(scores_filled, at(b, scores_filled, g * STEPS * GH))
                        load_products(b, g - 1 + NBUF)
                for h in range(2):
                    sp.wait_ge(*emptied(b, f"R1.{h}"))
                    sp.dma_start(out[b].rearrange("(t p) d -> p t d", p=P)[:, h * TH:(h + 1) * TH, :],
                                 x[:, h * TH:(h + 1) * TH, :]).then_inc(stored, 16)
            sp.wait_ge(stored, at(NB - 1, stored, 32))

        @block.gpsimd
        def _(pool):
            pool.memset(ident[:], 0.0).then_inc(zeroed, 1)
            pool.memset(vp[:], 0.0).then_inc(zeroed, 1)
            pool.memset(neghalf[:], -0.5).then_inc(consts, 1)
            pool.memset(ones[:], 1.0).then_inc(consts, 1)
            pool.memset(tiny[:], 1e-8).then_inc(consts, 1)
            pool.memset(one_pair[:], ONE_PAIR).then_inc(consts, 1)
            for e in range(NE):
                pool.memset(rank_of[:, e:e + 1], float(NE - e)).then_inc(consts, 1)
            pool.wait_ge(zeroed, 2)
            pool.affine_select(out=ident[:], in_=ident[:], compare_op=ALU.not_equal, fill=1.0, base=0,
                               pattern=[[-1, P]], channel_multiplier=1).then_inc(consts, 1)
            pool.memset(vp[:, :, :, HD:HD + 1], 1.0).then_inc(consts, 1)
            pool.wait_ge(consts, N_CONSTS)

            def rstds(b, n):
                for h in range(2):
                    pool.wait_ge(stats_ready, at(b, stats_ready, 2 * n + h + 1))
                    pool.tensor_tensor(rstd[:, h, :], veps[:, h, :], neghalf[:], ALU.pow).then_inc(rstd_ready, 1)

            with pool.Fori(0, NB) as b:
                pool.wait_ge(x0_used, at(b, x0_used, 0))
                pool.dma_start(x0[:], x_in[b].rearrange("(t p) d -> p t d", p=P)).then_inc(x_loaded, 16)
                rstds(b, N_REC)
                pool.wait_ge(rstd_ready, at(b, rstd_ready, 2))
                pool.tensor_tensor(mr[:].rearrange("p (h t) -> p h t", h=2), mv[:, :, 0].rearrange("p (h t) -> p h t", h=2), rstd[:, :, 0:TH], ALU.mult)
                pool.drain()
                for t in range(NT):
                    last = pool.tensor_scalar(z[:, t, :], x0[:, t, :], rstd[:, t // TH, t % TH:t % TH + 1], mr[:, t:t + 1], ALU.mult, ALU.subtract)
                last.then_inc(z_ready, 1)
                for n in (N_MLP, N_FFN0, N_ATTN):
                    rstds(b, n)
                pool.wait_ge(w_bias, 32)
                for g in range(NG):
                    if g:
                        pool.wait_ge(ring_filled, at(b, ring_filled, SLOT["bias", g - 1] + 1))
                    pool.tensor_tensor(varying[:], master[:, g * GH:(g + 1) * GH, ::-1], t_last[:, g * GH:(g + 1) * GH].unsqueeze(2).broadcast_to([P, GH, BIASW]),
                                       ALU.subtract).then_inc(varying_ready, 1)
                for n in (N_OUT, N_FFN1):
                    rstds(b, n)

        @block.scalar
        def _(act):
            def take(b, name, dst, func=ACT.Identity, signal=None, **kw):
                act.wait_ge(filled, at(b, filled, INDEX[name] + 1))
                act.activation(dst, banks[:, BANK[name], :], func, **kw).then_inc(signal or act_emptied, 1)

            def half(tile, h):
                return tile[:, h * HALF:(h + 1) * HALF]

            def ffn(b, f):
                for h in range(2):
                    take(b, f"T{f}.{h}", half(hT, h))
                act.wait_ge(logits_ready, at(b, logits_ready, f + 1))
                act.activation(ex[:], ls[:], ACT.Exp).then_inc(exps_ready, 1)
                act.wait_ge(second_ready, at(b, second_ready, f + 1))
                act.activation(e2[:], m2[:], ACT.Exp).then_inc(exp2_ready, 1)
                for h in range(2):
                    for k in range(2):
                        take(b, f"X{f}.{h}.{k}", half(umT[:, k, :], h))
                    for c in range(FC):
                        if h:
                            act.wait_ge(h_ready, at(b, h_ready, 2 * FC * f + c + 1))
                        take(b, f"HA{f}.{h}.{c}", h0[:, c, :], ACT.Relu, bias=bi[:, c:c + 1])
                for h in range(2):
                    take(b, f"O{f}.{h}", half(oT, h), bias=bo2[:])

            act.wait_ge(consts, N_CONSTS)
            act.activation(ks[64:96].rearrange("p n h t -> p (n h t)").bitcast(FP32), one_pair[64:96].broadcast_to([32, NBUF * GH * S // 2]), ACT.Copy).then_inc(k_ones, 1)
            act.wait_ge(w_rec, 16 * 6)
            act.wait_ge(w_mlp, 16 * 4)
            act.wait_ge(w_ffn, 16 * 7)
            act.wait_ge(bo2_ready, 1)
            act.nop().then_inc(act_emptied, CREDIT[act_emptied])
            with act.Fori(0, NB) as b:
                for h in range(2):
                    take(b, f"Trec.{h}", half(hT, h), scale=ln1_w[:])
                for h in range(2):
                    for c in range(REC):
                        take(b, f"XI.{h}.{c}", half(xinT[:, c, :], h))
                for h in range(2):
                    for c in range(REC):
                        take(b, f"G.{h}.{c}", half(gT[:, c, :], h), ACT.Sigmoid)
                for c in range(REC):
                    for h in range(2):
                        take(b, f"A.{h}.{c}", half(aT[:, c, :], h), ACT.Sigmoid, bias=a_param[:, c:c + 1])
                for c in range(REC):
                    act.wait_ge(one_minus_sq, at(b, one_minus_sq, c + 1))
                    act.activation(sT[:, c, :], sT[:, c, :], ACT.Sqrt, bias=tiny[:]).then_inc(root_ready, 1)
                for h in range(2):
                    take(b, f"WO.{h}", half(oT, h))
                for h in range(2):
                    take(b, f"Tmlp.{h}", half(hT, h), scale=ln2_w[:])
                for h in range(2):
                    for c in range(FC):
                        k = h * FC + c
                        if k >= 2:
                            act.wait_ge(*emptied(b, f"MG.{(k - 2) // FC}.{(k - 2) % FC}"))
                        take(b, f"MG.{h}.{c}", sg[:, k % 2, :], ACT.Sigmoid, signal=gate_sig)
                    take(b, f"MD.{h}", half(oT, h))
                ffn(b, 0)
                for h in range(2):
                    take(b, f"Tatt.{h}", half(hT, h))

                def mid(k):
                    act.wait_ge(*emptied(b, f"QK.{k // 2}.{k % 2}"))
                    act.activation(half(qk_part[:, k // 2, 1, :], k % 2), half(qk_rest[:, k // 2, :], k % 2), ACT.Copy).then_inc(qk_mid, 1)

                for k in range(4):
                    take(b, f"QK.{k // 2}.{k % 2}", half(qk_part[:, k // 2, 0, :], k % 2), ACT.Copy, signal=qk_high)
                    if k:
                        mid(k - 1)
                mid(3)

                def take_pv(g, q):
                    act.wait_ge(pv_done, at(b, pv_done, g * STEPS + STEPS - 1 + q))
                    if q == 0 and g:
                        act.wait_ge(ring_filled, at(b, ring_filled, SLOT["otr", g - 1] + 1))
                    act.activation(half(pvT, q), pv_bank(q), ACT.Copy).then_inc(pv_out, 1)

                for g in range(NG):
                    for s in range(STEPS):
                        step = g * STEPS + s
                        if step >= 2:
                            act.wait_ge(pv_done, at(b, pv_done, step - 1))
                        for h in range(GH):
                            n = step * GH + h
                            act.wait_ge(scores_filled, at(b, scores_filled, n + 1))
                            act.activation(probs[:, step % 2, h, :], score_bank(n), ACT.Exp, scale=SCALE).then_inc(exp_done, 1)
                            if h == 1 and s == STEPS - 1:
                                take_pv(g, 0)
                            if h == 1 and s == 0 and g:
                                take_pv(g - 1, 1)
                take_pv(NG - 1, 1)
                ffn(b, 1)

        @block.vector
        def _(dve):
            def bank(name, width=HALF):
                return banks[:, BANK[name], 0:width]

            def wait_filled(b, name):
                dve.wait_ge(filled, at(b, filled, INDEX[name] + 1))

            def tiles(h):
                return slice(h * TH, (h + 1) * TH)

            def stats_half(b, n, src, h):
                for t in range(h * TH, (h + 1) * TH):
                    dve.bn_stats(stats[:, t, :], src[:, t, :])
                dve.drain()
                for t in range(h * TH, (h + 1) * TH):
                    dve.bn_aggr(mv[:, t, :], stats[:, t, :])
                dve.drain()
                mean, var = mv[:, tiles(h), 0], mv[:, tiles(h), 1]
                if n == N_MLP:
                    dve.tensor_tensor(msq[:, tiles(h)], mean, mean, ALU.mult)
                    dve.drain()
                    dve.scalar_tensor_tensor(out=veps[:, h, 0:TH], in0=var, scalar=RMS_EPS, in1=msq[:, tiles(h)],
                                             op0=ALU.add, op1=ALU.add).then_inc(stats_ready, 1)
                elif n == N_REC:
                    dve.tensor_scalar(veps[:, h, 0:TH], var, LN_EPS, None, ALU.add)
                    dve.tensor_scalar(veps[:, h, TH:2 * TH], var, 1.0 + RMS_EPS, RMS_EPS * LN_EPS, ALU.mult, ALU.add).then_inc(stats_ready, 1)
                    dve.drain()
                else:
                    dve.tensor_scalar(veps[:, h, 0:TH], var, LN_EPS, None, ALU.add).then_inc(stats_ready, 1)

            def normed_half(b, n, src, h):
                dve.wait_ge(rstd_ready, at(b, rstd_ready, 2 * n + h + 1))
                for t in range(h * TH, (h + 1) * TH):
                    r = rstd[:, h, t % TH:t % TH + 1] if n != N_REC else rstd[:, h, TH + t % TH:TH + t % TH + 1]
                    if n == N_MLP:
                        last = dve.tensor_scalar(nt[:, t, :], src[:, t, :], r, None, ALU.mult)
                    else:
                        last = dve.tensor_scalar(nt[:, t, :], src[:, t, :], mv[:, t, 0:1], r, ALU.subtract, ALU.mult)
                if n in TRANSPOSED:
                    last.then_inc(norm_ready, 1)

            def norm(b, n, src):
                for h in range(2):
                    stats_half(b, n, src, h)
                for h in range(2):
                    normed_half(b, n, src, h)

            def per_tile(v):
                return v[:].unsqueeze(2).broadcast_to([P, NT, NE])

            ranks = rank_of[:].unsqueeze(1).broadcast_to([P, NT, NE])

            def first_of(scores, top, k, pick):
                dve.tensor_tensor(key[:], scores[:], top, ALU.is_equal)
                dve.drain()
                dve.tensor_tensor(key[:], key[:], ranks, ALU.mult)
                dve.drain()
                dve.tensor_reduce(k[:], key[:], axis=AXX, op=ALU.max)
                dve.drain()
                dve.tensor_tensor(pick[:], ranks, per_tile(k), ALU.is_equal)
                dve.drain()

            def ffn(b, f):
                n = (N_FFN0, N_FFN1)[f]
                dve.drain()
                norm(b, n, x)
                for j in range(NT // 2):
                    wait_filled(b, f"U{f}.{j}")
                    u = bank(f"U{f}.{j}", 2 * UW).rearrange("p (t c) -> p t c", c=UW)
                    dve.tensor_tensor(lg[:, 2 * j:2 * j + 2, :], u[:, :, P:UW], gate_b[:].unsqueeze(1).broadcast_to([P, 2, NE]), ALU.add)
                dve.drain()
                dve.tensor_reduce(m1[:], lg[:], axis=AXX, op=ALU.max)
                dve.drain()
                dve.tensor_tensor(ls[:], lg[:], per_tile(m1), ALU.subtract)
                dve.drain()
                dve.tensor_scalar(ls[:], ls[:], UNDERFLOW, None, ALU.max).then_inc(logits_ready, 1)
                dve.drain()
                first_of(ls, per_tile(zero_t), k1, pick0)
                dve.scalar_tensor_tensor(out=ls2[:].rearrange("p t e -> p (t e)"), in0=pick0[:].rearrange("p t e -> p (t e)"), scalar=-1e30,
                                         in1=ls[:].rearrange("p t e -> p (t e)"), op0=ALU.mult, op1=ALU.add)
                dve.drain()
                dve.tensor_reduce(m2[:], ls2[:], axis=AXX, op=ALU.max).then_inc(second_ready, 1)
                dve.drain()
                first_of(ls2, per_tile(m2), k2, pick1)
                dve.tensor_tensor(pickd[:], pick1[:], pick0[:], ALU.subtract)
                dve.drain()
                for j in range(NT // 2):
                    u = bank(f"U{f}.{j}", 2 * UW).rearrange("p (t c) -> p t c", c=UW)[:, :, 0:P].rearrange("p t (e r) -> p t e r", r=RANK)
                    for k, pick in enumerate((pick0, pickd)):
                        last = dve.tensor_tensor(um[:, k, 2 * j:2 * j + 2, :].rearrange("p t (e r) -> p t e r", r=RANK), u,
                                                 pick[:, 2 * j:2 * j + 2, :].unsqueeze(3).broadcast_to([P, 2, NE, RANK]), ALU.mult)
                    last.then_inc(dve_emptied, 1)
                dve.wait_ge(exps_ready, at(b, exps_ready, f + 1))
                dve.tensor_reduce(esum[:], ex[:], axis=AXX, op=ALU.add)
                dve.drain()
                dve.reciprocal(ersum[:], esum[:])
                dve.drain()
                dve.wait_ge(exp2_ready, at(b, exp2_ready, f + 1))
                dve.scalar_tensor_tensor(out=val[:], in0=e2[:], scalar=1.0, in1=ersum[:], op0=ALU.add, op1=ALU.mult)
                for h in range(2):
                    for c in range(FC):
                        wait_filled(b, f"HB{f}.{h}.{c}")
                        dve.tensor_scalar(h1[:, c % 2, :], bank(f"HB{f}.{h}.{c}"), bi[:, c:c + 1], 0.0, ALU.add, ALU.max).then_inc(dve_emptied, 1)
                        dve.wait_ge(*emptied(b, f"HB{f}.{h}.{c}"))
                        dve.tensor_tensor(hs[:, c, h * HALF:(h + 1) * HALF], h1[:, c % 2, :], h0[:, c, :], ALU.add).then_inc(h_ready, 1)
                for h in range(2):
                    wait_filled(b, f"R{f}.{h}")
                    for t in range(h * TH, (h + 1) * TH):
                        last = dve.scalar_tensor_tensor(out=x[:, t, :], in0=bank(f"R{f}.{h}")[:, (t % TH) * P:(t % TH + 1) * P], scalar=val[:, t:t + 1],
                                                        in1=x[:, t, :], op0=ALU.mult, op1=ALU.add)
                    last.then_inc(dve_emptied, 1)

            dve.memset(zero_t[:], 0.0)
            dve.wait_ge(w_ffn, 16 * 7)
            dve.wait_ge(w_att, 16 * 3)
            dve.wait_ge(w_bias, 32)
            dve.wait_ge(consts, N_CONSTS)
            dve.tensor_scalar(bo2[:], bo[:], 2.0, None, ALU.mult).then_inc(bo2_ready, 1)
            dve.nop().then_inc(dve_emptied, CREDIT[dve_emptied])
            dve.nop().then_inc(x0_used, CREDIT[x0_used])
            with dve.Fori(0, NB) as b:
                dve.wait_ge(x_loaded, b * 16 + 16)
                norm(b, N_REC, x0)
                for c in range(REC):
                    dve.wait_ge(*emptied(b, f"A.1.{c}"))
                    dve.tensor_tensor(sT[:, c, :], aT[:, c, :], aT[:, c, :], ALU.mult)
                    dve.drain()
                    dve.tensor_scalar(sT[:, c, :], sT[:, c, :], -1.0, 1.0, ALU.mult, ALU.add).then_inc(one_minus_sq, 1)
                for c in range(REC):
                    dve.wait_ge(root_ready, at(b, root_ready, c + 1))
                    dve.tensor_tensor(sT[:, c, :], sT[:, c, :], xinT[:, c, :], ALU.mult)
                    dve.drain()
                    dve.tensor_tensor_scan(yT[:, c, :], aT[:, c, :], sT[:, c, :], 0.0, ALU.mult, ALU.add)
                    dve.drain()
                    dve.tensor_tensor(yT[:, c, :], yT[:, c, :], gT[:, c, :], ALU.mult).then_inc(y_ready, 1)
                dve.wait_ge(z_ready, at(b, z_ready, 1))
                for h in range(2):
                    wait_filled(b, f"Rrec.{h}")
                    dve.tensor_tensor(x1[:, tiles(h), :], z[:, tiles(h), :], bank(f"Rrec.{h}").rearrange("p (t d) -> p t d", d=P), ALU.add).then_inc(dve_emptied, 1)
                    dve.drain()
                    stats_half(b, N_MLP, x1, h)
                for h in range(2):
                    normed_half(b, N_MLP, x1, h)
                dve.wait_ge(stored, at(b, stored, 0))
                dve.tensor_tensor(x[:], x0[:], x1[:], ALU.add).then_inc(x0_used, 1)
                for h in range(2):
                    for c in range(FC):
                        k = h * FC + c
                        dve.wait_ge(gate_sig, at(b, gate_sig, k + 1))
                        dve.tensor_tensor(sgu[:, k % 2, :], sg[:, k % 2, :], bank(f"MG.{h}.{c}"), ALU.mult).then_inc(dve_emptied, 1)
                        wait_filled(b, f"MU.{h}.{c}")
                        dve.wait_ge(*emptied(b, f"MG.{h}.{c}"))
                        dve.tensor_tensor(m_T[:, c, h * HALF:(h + 1) * HALF], sgu[:, k % 2, :], bank(f"MU.{h}.{c}"), ALU.mult).then_inc(dve_emptied, 1)
                for h in range(2):
                    wait_filled(b, f"Rmlp.{h}")
                    dve.tensor_tensor(x[:, tiles(h), :], x[:, tiles(h), :], bank(f"Rmlp.{h}").rearrange("p (t d) -> p t d", d=P), ALU.add).then_inc(dve_emptied, 1)
                ffn(b, 0)
                dve.drain()
                norm(b, N_ATTN, x)

                def part_of(k, i):
                    return qk_part[:, k // 2, i, (k % 2) * HALF:(k % 2 + 1) * HALF]

                def rest_of(k):
                    return qk_rest[:, k // 2, (k % 2) * HALF:(k % 2 + 1) * HALF]

                def low(k):
                    dve.wait_ge(qk_mid, at(b, qk_mid, k + 1))
                    dve.tensor_tensor(part_of(k, 2), rest_of(k), part_of(k, 1), ALU.subtract).then_inc(qk_low, 1)

                for k in range(4):
                    dve.wait_ge(qk_high, at(b, qk_high, k + 1))
                    dve.tensor_tensor(rest_of(k), bank(f"QK.{k // 2}.{k % 2}"), part_of(k, 0), ALU.subtract).then_inc(dve_emptied, 1)
                    if k:
                        low(k - 1)
                low(3)
                for h in range(2):
                    wait_filled(b, f"V.{h}")
                    dve.tensor_copy(vp[:, tiles(h), :, 0:HD], bank(f"V.{h}").rearrange("p (t h d) -> p t h d", h=NH, d=HD)).then_inc(dve_emptied, 1)
                wait_filled(b, "CS")
                dve.tensor_tensor(cs[:].rearrange("p (h d) -> p h d", d=HD), bank("CS", P).rearrange("p (h d) -> p h d", d=HD),
                                  t_last[:].unsqueeze(2).broadcast_to([P, NH, HD]), ALU.mult).then_inc(dve_emptied, 1)

                for n, item in enumerate(RING):
                    kind, g = item[0], item[1]
                    slot = ring(item)
                    heads = slice(g * GH * HD, (g + 1) * GH * HD)
                    dve.wait_ge(ring_filled, at(b, ring_filled, n + 1))
                    if kind == "max":
                        dve.tensor_reduce(negmax[:, g % 2, item[2]:item[2] + 1], slot.rearrange("p a b -> p (a b)"), axis=AXX, op=ALU.max,
                                          negate=True).then_inc(ring_emptied, 1)
                    elif kind == "mtr":
                        rows = slot[0:GH * NT, 0, 0:P]
                        dve.tensor_copy(nm_part[:, g % 2, 0, :], rows)
                        dve.drain()
                        dve.tensor_tensor(nm_rest[:], rows, nm_part[:, g % 2, 0, :], ALU.subtract).then_inc(ring_emptied, 1)
                        dve.drain()
                        dve.tensor_copy(nm_part[:, g % 2, 1, :], nm_rest[:])
                        dve.drain()
                        dve.tensor_tensor(nm_part[:, g % 2, 2, :], nm_rest[:], nm_part[:, g % 2, 1, :], ALU.subtract).then_inc(negmax_split, 1)
                    elif kind == "bias":
                        dve.tensor_copy(biasT[:], slot[:, 0, :]).then_inc(ring_emptied, 1)
                    elif kind == "otr":
                        o = slot.rearrange("p a (t g v) -> p (a t) g v", g=GH, v=VW)
                        dve.reciprocal(rl[:], o[:, :, :, HD])
                        dve.drain()
                        dve.tensor_tensor(o_tok[:, :, heads].rearrange("p t (g d) -> p t g d", d=HD), o[:, :, :, 0:HD],
                                          rl[:].unsqueeze(3).broadcast_to([P, NT, GH, HD]), ALU.mult).then_inc(ring_emptied, 1)
                        dve.drain()
                    elif kind == "btr":
                        o = slot[:, 0, :].rearrange("p (t g v) -> p t g v", g=GH, v=VW)
                        dst = o_tok[:, 0:TH, heads].rearrange("p t (g d) -> p t g d", d=HD)
                        dve.tensor_tensor(dst, dst, o[:, :, :, 0:HD], ALU.add).then_inc(ring_emptied, 1)
                dve.drain()
                dve.tensor_tensor(o_tok[:], o_tok[:], cs[:].unsqueeze(1).broadcast_to([P, NT, P]), ALU.add)
                dve.drain()
                norm(b, N_OUT, o_tok)
                dve.drain()
                for op, tile in ((ALU.mult, gamma), (ALU.add, beta)):
                    dve.tensor_tensor(nt[:], nt[:], tile[:].unsqueeze(1).broadcast_to([P, NT, P]), op)
                    dve.drain()
                dve.tensor_tensor(x[:], x[:], nt[:], ALU.add)
                ffn(b, 1)

        @block.tensor
        def _(pe):
            def begin(b, name):
                if BEFORE[name]:
                    pe.wait_ge(*emptied(b, BEFORE[name]))
                else:
                    pe.wait_ge(act_emptied, at(b, act_emptied, 0))
                    pe.wait_ge(dve_emptied, at(b, dve_emptied, 0))

            def dense(b, name, terms, start=True, stop=True):
                begin(b, name)
                for i, (lhsT, rhs) in enumerate(terms):
                    last = pe.matmul(banks[:, BANK[name], :], lhsT, rhs, start=start and i == 0, stop=stop and i == len(terms) - 1)
                last.then_inc(filled, 1)

            def flip(b, name, blocks):
                begin(b, name)
                for i, src in enumerate(blocks):
                    last = pe.transpose(banks[:, BANK[name], i * P:(i + 1) * P], src, ident[:])
                last.then_inc(filled, 1)

            def half(tile, h):
                return tile[:, h * HALF:(h + 1) * HALF]

            def chunk(tile, c):
                return tile[:, c * P:(c + 1) * P]

            def norm_T(b, n, prefix):
                for h in range(2):
                    pe.wait_ge(norm_ready, at(b, norm_ready, 2 * TRANSPOSED[n] + h + 1))
                    flip(b, f"{prefix}.{h}", [nt[:, h * TH + i, :] for i in range(TH)])

            def back(b, src_job, job):
                for h in range(2):
                    pe.wait_ge(*emptied(b, f"{src_job}.{h}"))
                    flip(b, f"{job}.{h}", [chunk(oT, h * TH + i) for i in range(TH)])

            def ffn(b, f):
                norm_T(b, (N_FFN0, N_FFN1)[f], f"T{f}")
                for j in range(NT // 2):
                    name = f"U{f}.{j}"
                    pe.wait_ge(*emptied(b, f"T{f}.{j // 2}"))
                    begin(b, name)
                    for i in range(2):
                        last = pe.matmul(banks[:, BANK[name], i * UW:(i + 1) * UW], chunk(hT, 2 * j + i), agT[:], start=True, stop=True)
                    last.then_inc(filled, 1)

                def base(h, c):
                    begin(b, f"HA{f}.{h}.{c}")
                    pe.matmul(banks[:, BANK[f"HA{f}.{h}.{c}"], :], chunk(wiT, c), half(hT, h), start=True, stop=False, skip_group_check=True)

                def lora(name, h, c, k):
                    pe.matmul(banks[:, BANK[name], :], chunk(bT, c), half(umT[:, k, :], h), start=False, stop=k == 1, skip_group_check=True).then_inc(filled, 1)

                for h in range(2):
                    if h == 0:
                        base(0, 0)
                        base(0, 1)
                        pe.wait_ge(*emptied(b, f"U{f}.3"))
                    for k in range(2):
                        flip(b, f"X{f}.{h}.{k}", [um[:, k, h * TH + i, :] for i in range(TH)])
                    for c in range(FC):
                        if h or c >= 2:
                            base(h, c)
                        if c == 0:
                            pe.wait_ge(*emptied(b, f"X{f}.{h}.1"))
                        lora(f"HA{f}.{h}.{c}", h, c, 0)
                    for c in range(FC):
                        pe.wait_ge(*emptied(b, f"HA{f}.{h}.{c}"))
                        lora(f"HB{f}.{h}.{c}", h, c, 1)
                for h in range(2):
                    pe.wait_ge(h_ready, at(b, h_ready, 2 * FC * f + FC * (h + 1)))
                    dense(b, f"O{f}.{h}", [(woT[:, c, :], half(hs[:, c, :], h)) for c in range(FC)])
                back(b, f"O{f}", f"R{f}")

            pe.wait_ge(consts, N_CONSTS)
            pe.wait_ge(w_rec, 16 * 6)
            pe.wait_ge(w_mlp, 16 * 4)
            pe.wait_ge(w_ffn, 16 * 7)
            pe.wait_ge(w_att, 16 * 3)
            with pe.Fori(0, NB) as b:
                norm_T(b, N_REC, "Trec")
                for h in range(2):
                    pe.wait_ge(*emptied(b, f"Trec.{h}"))
                    for c in range(REC):
                        dense(b, f"XI.{h}.{c}", [(chunk(w_inT, c), half(hT, h))])
                for h in range(2):
                    for c in range(REC):
                        dense(b, f"G.{h}.{c}", [(chunk(w_gateT, c), half(hT, h))])
                for c in range(REC):
                    for h in range(2):
                        pe.wait_ge(*emptied(b, f"XI.{h}.1"))
                        dense(b, f"A.{h}.{c}", [(chunk(w_aT[:, k, :], c), half(xinT[:, k, :], h)) for k in range(REC)])
                pe.wait_ge(y_ready, at(b, y_ready, REC))
                for h in range(2):
                    dense(b, f"WO.{h}", [(w_outT[:, k, :], half(yT[:, k, :], h)) for k in range(REC)])
                back(b, "WO", "Rrec")
                norm_T(b, N_MLP, "Tmlp")
                for h in range(2):
                    pe.wait_ge(*emptied(b, f"Tmlp.{h}"))
                    for c in range(FC):
                        dense(b, f"MG.{h}.{c}", [(chunk(mgT, c), half(hT, h))])
                        dense(b, f"MU.{h}.{c}", [(chunk(muT, c), half(hT, h))])
                    pe.wait_ge(*emptied(b, f"MU.{h}.{FC - 1}"))
                    dense(b, f"MD.{h}", [(mdT[:, c, :], half(m_T[:, c, :], h)) for c in range(FC)])
                back(b, "MD", "Rmlp")
                ffn(b, 0)
                norm_T(b, N_ATTN, "Tatt")
                pe.wait_ge(*emptied(b, "Tatt.1"))
                for which in range(2):
                    for h in range(2):
                        dense(b, f"QK.{which}.{h}", [(wqkvT[:, which, :], half(hT, h))])
                for h in range(2):
                    name = f"V.{h}"
                    begin(b, name)
                    for i in range(TH):
                        last = pe.matmul(banks[:, BANK[name], i * P:(i + 1) * P], chunk(hT, h * TH + i), wqkvT[:, 2, :], start=True, stop=True)
                    last.then_inc(filled, 1)
                begin(b, "CS")
                pe.wait_ge(*emptied(b, "V.1"))
                for t in range(NT):
                    last = pe.matmul(banks[:, BANK["CS"], 0:P], ones[:], vp[:, t, :, 0:HD], start=t == 0, stop=t == NT - 1)
                last.then_inc(filled, 1)
                pe.wait_ge(*emptied(b, "CS"))

                def ring_item(item):
                    n, kind, g = SLOT[item], item[0], item[1]
                    slot = ring(item)
                    if n >= 2:
                        pe.wait_ge(ring_emptied, at(b, ring_emptied, n - 1))
                    if kind == "max":
                        h, t = item[2] // NT, item[2] % NT
                        if item[2] == 0:
                            groups = len(range(g % NBUF, NG, NBUF))
                            pe.wait_ge(qk_loaded[g % NBUF], (b * groups + g // NBUF + 1) * 16 * 2 * NPART * NPART)
                        for k in range(2):
                            last = pe.matmul(slot[:, k, :], qs[0:STACK, g % NBUF, h, t * P:(t + 1) * P], ks[0:STACK, g % NBUF, h, k * HALF:(k + 1) * HALF],
                                             start=True, stop=True)
                    elif kind == "mtr":
                        pe.wait_ge(ring_emptied, at(b, ring_emptied, SLOT["max", g, MAXES - 1] + 1))
                        last = pe.transpose(slot[0:GH * NT, 0, 0:P], negmax[:, g % 2, :], ident[:])
                    elif kind == "bias":
                        pe.wait_ge(varying_ready, at(b, varying_ready, g + 1))
                        for t in range(NT - 1, TH - 1, -1):
                            skip = (NT - 1 - t) * P
                            for h in range(GH):
                                last = pe.matmul(slot[32 * h:32 * h + VW, 0, 0:BIASW - skip], vp[:, t, g * GH + h, :], varying[:, h, skip:BIASW],
                                                 start=t == NT - 1, stop=t == TH)
                    elif kind == "otr":
                        pe.wait_ge(pv_out, at(b, pv_out, 2 * g + 2))
                        for t in range(NT):
                            last = pe.transpose(slot[:, t // TH, (t % TH) * P:(t % TH + 1) * P], chunk(pvT, t), ident[:])
                    elif kind == "btr":
                        pe.wait_ge(ring_emptied, at(b, ring_emptied, SLOT["bias", g] + 1))
                        for t in range(TH):
                            last = pe.transpose(slot[:, 0, t * P:(t + 1) * P], chunk(biasT, t), ident[:])
                    last.then_inc(ring_filled, 1)

                def scores(g, s, h):
                    n = (g * STEPS + s) * GH + h
                    if n >= 2:
                        pe.wait_ge(exp_done, at(b, exp_done, n - 1))
                    if s == 0 and h == 0:
                        pe.wait_ge(negmax_loaded[g], b * 16 * NPART + 16 * NPART)
                    t, q = s // 2, s % 2
                    pe.matmul(score_bank(n), ks[0:DEPTH, g % NBUF, h, t * P:(t + 1) * P], qs[0:DEPTH, g % NBUF, h, q * HALF:(q + 1) * HALF],
                              start=True, stop=True).then_inc(scores_filled, 1)

                def weigh(step):
                    g, s = step // STEPS, step % STEPS
                    t, q = s // 2, s % 2
                    pe.wait_ge(exp_done, at(b, exp_done, (step + 1) * GH))
                    if t == 0 and g:
                        pe.wait_ge(pv_out, at(b, pv_out, 2 * (g - 1) + q + 1))
                    for h in range(GH):
                        last = pe.matmul(pv_bank(q)[32 * h:32 * h + VW, :], vp[:, t, g * GH + h, :], probs[:, step % 2, h, :],
                                         start=t == 0, stop=t == NT - 1)
                    last.then_inc(pv_done, 1)

                for n in range(MAXES):
                    ring_item(("max", 0, n))
                ring_item(("mtr", 0))
                for g in range(NG):
                    for s in range(STEPS):
                        step = g * STEPS + s
                        items = ring_items(g, s)
                        scores(g, s, 0)
                        for item in items[:1]:
                            ring_item(item)
                        scores(g, s, 1)
                        if step:
                            weigh(step - 1)
                        scores(g, s, 2)
                        for item in items[1:2]:
                            ring_item(item)
                        scores(g, s, 3)
                        for item in items[2:]:
                            ring_item(item)
                weigh(NG * STEPS - 1)
                ring_item(("otr", NG - 1))
                ring_item(("btr", NG - 1))
                ffn(b, 1)
    return nc


def kernel(**inputs):
    import concourse.bacc as bacc
    from concourse.bass_utils import run_bass_kernel_spmd

    a = {k[3:]: np.asarray(v) for k, v in inputs.items()}

    def col(v, n=1):
        return v.reshape(n, P).T

    clipped = np.minimum(np.arange(P - 1 + BIASW), LAST)
    laid = {
        "x": a["attn_a_x"], "ln1_w": col(a["attn_a_ln1_w"]), "ln2_w": col(a["attn_a_ln2_w"]),
        "w_inT": a["attn_a_w_in"].T, "w_gateT": a["attn_a_w_gate"].T, "w_aT": a["attn_a_w_a"].T, "w_outT": a["attn_a_w_out"].T,
        "a_param": col(a["attn_a_a_param"], REC), "mgT": a["attn_a_w_mlp_gate"].T, "muT": a["attn_a_w_mlp_up"].T,
        "mdT": a["attn_a_w_mlp_down"].T,
        "wqkvT": np.concatenate([a["attn_b_Wq"].T, a["attn_b_Wk"].T, a["attn_b_Wv"].T]),
        "tab": a["attn_b_rel_bias_table"].T[:, clipped[::-1]],
        "t_last": a["attn_b_rel_bias_table"][LAST:LAST + 1],
        "gamma": a["attn_b_ln_gamma"].reshape(1, P), "beta": a["attn_b_ln_beta"].reshape(1, P),
        "wiT": a["ffn_wi"].T, "bi": col(a["ffn_bi"], FC), "woT": a["ffn_wo"].T, "bo": col(a["ffn_bo"]),
        "agT": np.concatenate([a["ffn_lora_A"].reshape(P, P), a["ffn_gate_w"]]).T,
        "bT": a["ffn_lora_B"].transpose(0, 2, 1).reshape(P, FC * P), "gate_b": a["ffn_gate_b"].reshape(1, NE),
    }
    nc = bacc.Bacc("TRN2", target_bir_lowering=False, num_devices=1)
    arrays, aps = {}, {}
    for name, v in laid.items():
        arrays[f"in_{name}"] = np.ascontiguousarray(v)
        aps[name] = nc.dram_tensor(f"in_{name}", v.shape, FP32, kind="ExternalInput").ap()
    out = nc.dram_tensor("out", (NB, S, P), FP32, kind="ExternalOutput").ap()
    build(nc, aps.pop("x"), out, aps, aps.pop("tab"))
    return run_bass_kernel_spmd(nc, [arrays], core_ids=[0]).results[0]["out"]
```

```python
import numpy as np
import concourse.bass as bass
from concourse import mybir
from contextlib import ExitStack

FP32 = mybir.dt.float32
BF16 = mybir.dt.bfloat16
ALU = mybir.AluOpType
ACT = mybir.ActivationFunctionType
AXX = mybir.AxisListType.X

P = 128
NB = 2
S = 1024
NT = S // P
HALF = S // 2
TH = NT // 2
BLOCKS = [(b, h) for b in range(NB) for h in range(2)]
REC = 2
FC = 4
NE, RANK = 8, 16
UW = P + NE
NH, HD = 16, 8
GH = 4
GW = GH * HD
NG = NH // GH
GROUPS = NB * NG
NPART = 3
STACK = NPART * NPART * HD
DEPTH = STACK + NPART
VW = 32
BIASW = 512
LAST = 510
LN_EPS, RMS_EPS = 1e-5, 1e-6
SCALE = float(P) ** -0.5
UNDERFLOW = -87.336544
N_CONSTS = 5 + NE
ONE_PAIR = float(np.array([0x3F803F80], np.uint32).view(np.float32)[0])

N_REC, N_MLP, N_FFN0, N_ATTN, N_OUT, N_FFN1 = range(6)
NORMS = [(n, b) for n in range(4) for b in range(NB)] + [(n, b) for b in range(NB) for n in (N_OUT, N_FFN1)]
NORM_AT = {nb: i for i, nb in enumerate(NORMS)}
FLIPPED_AT = {nb: i for i, nb in enumerate(x for x in NORMS if x[0] != N_OUT)}


def ffn_order(f):
    jobs = []
    jobs += [(f"T{f}.0.{h}", "act") for h in range(2)] + [(f"U{f}.0.{j}", "dve") for j in range(4)]
    jobs += [(f"T{f}.1.{h}", "act") for h in range(2)]
    for q in range(len(BLOCKS) + 2):
        if q < 4:
            b, h = BLOCKS[q]
            jobs += [(f"X{f}.{b}.{h}.{k}", "act") for k in range(2)]
            jobs += [(f"HA{f}.{b}.{h}.{c}", "act") for c in range(FC)]
            jobs += [(f"HB{f}.{b}.{h}.{c}", "dve") for c in range(FC)]
        if q == 0:
            jobs += [(f"U{f}.1.{j}", "dve") for j in range(4)]
        if 1 <= q < 5:
            jobs.append(("O%d.%d.%d" % (f, *BLOCKS[q - 1]), "act"))
        if q >= 2:
            jobs.append(("R%d.%d.%d" % (f, *BLOCKS[q - 2]), "dve"))
    return jobs


def dense_order():
    jobs = []
    for b in range(NB):
        jobs += [(f"Trec.{b}.{h}", "act") for h in range(2)]
        for kind in ("XI", "G", "A"):
            for x, y in ((0, 0), (0, 1), (1, 0), (1, 1)):
                h, c = (y, x) if kind == "A" else (x, y)
                jobs.append((f"{kind}.{b}.{h}.{c}", "act"))
    for b in range(NB):
        jobs += [(f"WO.{b}.{h}", "act") for h in range(2)]
        jobs += [(f"Rrec.{b}.{h}", "dve") for h in range(2)]
    for b in range(NB):
        jobs += [(f"Tmlp.{b}.{h}", "act") for h in range(2)]
    for q in range(len(BLOCKS) + 2):
        if q < 4:
            b, h = BLOCKS[q]
            for c in range(FC):
                jobs += [(f"MG.{b}.{h}.{c}", "dve"), (f"MU.{b}.{h}.{c}", "dve")]
        if 1 <= q < 5:
            jobs.append(("MD.%d.%d" % BLOCKS[q - 1], "act"))
        if q >= 2:
            jobs.append(("Rmlp.%d.%d" % BLOCKS[q - 2], "dve"))
    jobs += ffn_order(0)
    for b in range(NB):
        jobs += [(f"Tatt.{b}.{h}", "act") for h in range(2)]
        jobs += [(f"QK.{b}.{w}.{h}", "dve") for w in range(2) for h in range(2)]
    for b in range(NB):
        jobs += [(f"V.{b}.{h}", "dve") for h in range(2)]
        jobs.append((f"CS.{b}", "dve"))
    return jobs + ffn_order(1)


def assign_banks(order):
    bank, turn = {}, 0
    for name, _ in order:
        if name.startswith("HB"):
            bank[name] = bank["HA" + name[2:]]
        else:
            bank[name] = turn % 8
            turn += 1
    return bank


JOBS = dense_order()
BANK = assign_banks(JOBS)
INDEX = {name: i for i, (name, _) in enumerate(JOBS)}
EMPTYING = {name: (c, sum(x[1] == c for x in JOBS[: i + 1])) for i, (name, c) in enumerate(JOBS)}
BEFORE = {name: ([None] + [n for n, _ in JOBS[:i] if BANK[n] == BANK[name]])[-1] for i, (name, _) in enumerate(JOBS)}

STEPS = 2 * NT
MAXES = GH * NT
LEAD = MAXES + 1
PER_GROUP_RING = MAXES + 4
MTR, BIAS, BTR, OTR = range(MAXES, MAXES + 4)
LAST_RING = 3


def build(nc, x_in, out, w, tab):
    ctx = ExitStack()
    with ctx:
        def sb(name, shape, dt=FP32):
            return ctx.enter_context(nc.sbuf_tensor(name, shape, dt))

        def sem(name):
            return ctx.enter_context(nc.semaphore(name))

        w_inT = sb("w_inT", [P, REC * P])
        w_gateT = sb("w_gateT", [P, REC * P])
        w_aT = sb("w_aT", [P, REC, REC * P])
        w_outT = sb("w_outT", [P, REC, P])
        mgT = sb("mgT", [P, FC * P])
        muT = sb("muT", [P, FC * P])
        mdT = sb("mdT", [P, FC, P])
        a_param = sb("a_param", [P, REC])
        ln1_w = sb("ln1_w", [P, 1])
        ln2_w = sb("ln2_w", [P, 1])
        wiT = sb("wiT", [P, FC * P])
        bi = sb("bi", [P, FC])
        woT = sb("woT", [P, FC, P])
        bo = sb("bo", [P, 1])
        bo2 = sb("bo2", [P, 1])
        agT = sb("agT", [P, UW])
        bT = sb("bT", [P, FC * P])
        gate_b = sb("gate_b", [P, NE])
        wqkvT = sb("wqkvT", [P, 3, P])
        gamma = sb("gamma", [P, P])
        beta = sb("beta", [P, P])
        t_last = sb("t_last", [P, GROUPS * GH])
        ident = sb("ident", [P, P])
        ones = sb("ones", [P, P])
        rank_of = sb("rank_of", [P, NE])
        one_pair = sb("one_pair", [P, 1])
        neghalf = sb("neghalf", [P, 2 * TH])
        tiny = sb("tiny", [P, 1])
        zero_t = sb("zero_t", [P, NT])

        x0 = sb("x0", [P, NB, NT, P])
        x = sb("x", [P, NB, NT, P])
        z = sb("z", [P, NB, NT, P])
        x1 = sb("x1", [P, NB, NT, P])
        nt = sb("nt", [P, NB, NT, P])
        v_all = x1[:].rearrange("p b t c -> p (b t c)").rearrange("p (g t c) -> p g t c", g=GROUPS, t=NT)
        o_tok = z[:].rearrange("p b t c -> p (b t c)").rearrange("p (g t c) -> p g t c", g=GROUPS, t=NT)
        stats = sb("stats", [P, NB, NT, 6])
        mv = sb("mv", [P, NB, NT, 2])
        veps = sb("veps", [P, NB, 2, 2 * TH])
        rstd = sb("rstd", [P, NB, 2, 2 * TH])
        msq = sb("msq", [P, NB, NT])
        hT = sb("hT", [P, NB, S])
        oT = sb("oT", [P, NB, S])

        DENSE = 11 * S
        TAIL = 8 * S
        arena = sb("arena", [P, NB * DENSE + TAIL])

        def carve(start, *shapes):
            tiles_ = []
            for shape in shapes:
                size = 1
                for n in shape:
                    size *= n
                flat = arena[:, start:start + size]
                axes = " ".join(f"a{i}" for i in range(len(shape)))
                tiles_.append(flat.rearrange(f"p ({axes}) -> p {axes}", **{f"a{i}": n for i, n in enumerate(shape)}) if len(shape) > 1 else flat)
                start += size
            return tiles_

        rec, mlp, moe = [], [], []
        for b in range(NB):
            rec.append(carve(b * DENSE, *[[REC, S]] * 5))
            mlp.append(carve(b * DENSE, [2, HALF], [2, HALF], [FC, S]))
            moe.append(carve(b * DENSE, [FC, HALF], [2, HALF], [FC, S], [2, NT, P], [2, S]))
        probs, q_words, pvT, biasT, qk_rest, qk_words, varying = carve(
            0, [2, GH, HALF], [2 * GH * S // 2], [S], [BIASW], [NB, 2, S], [NB * 2 * NPART * S // 2], [GH, BIASW])
        qs = q_words.bitcast(BF16).rearrange("p (n h t) -> p n h t", n=2, h=GH)
        qk_part = qk_words.bitcast(BF16).rearrange("p (b w n t) -> p b w n t", b=NB, w=2, n=NPART)
        k_words, vpg, bias_raw = carve(NB * DENSE, [2 * GH * S // 2], [2, NT, GH, VW], [GH, BIASW])
        ks = k_words.bitcast(BF16).rearrange("p (n h t) -> p n h t", n=2, h=GH)
        lg, ls, ls2, ex, key, pick0, pick1, pickd = (sb(n, [P, NB, NT, NE]) for n in
                                                     ("lg", "ls", "ls2", "ex", "key", "pick0", "pick1", "pickd"))
        m1, m2, k1, k2, esum, ersum, e2, val = (sb(n, [P, NB, NT]) for n in ("m1", "m2", "k1", "k2", "esum", "ersum", "e2", "val"))
        cs = sb("cs", [P, NB, P])
        negmax = sb("negmax", [P, 2, GH * NT])
        nm_rest = sb("nm_rest", [GH * NT, P])
        nm_part = sb("nm_part", [GH * NT, 2, NPART, P], BF16)
        rl = sb("rl", [P, NT, GH])
        bias_tok = sb("bias_tok", [P, TH, GH, HD])
        pause = sb("pause", [P, 2 * TH])

        scratch = nc.dram_tensor("qk_scratch", (2, NPART, NB * P, S), BF16, kind="Internal").ap()
        banks = ctx.enter_context(nc.psum_tensor("banks", [P, 8, HALF], FP32))

        def slot_of(n):
            return banks[:, 2 * (n % 2):2 * (n % 2) + 2, :]

        def score_bank(n):
            return banks[:, 4 + n % 3, :]

        pv_bank = banks[:, 7, :]

        w_small = sem("w_small")
        w_rec, w_mlp, w_ffn, w_att, bo2_ready, k_ones = (sem(n) for n in ("w_rec", "w_mlp", "w_ffn", "w_att", "bo2_ready", "k_ones"))
        zeroed, consts, v_ones = sem("zeroed"), sem("consts"), sem("v_ones")
        x_loaded = [sem(f"x_loaded{b}") for b in range(NB)]
        z_ready, stored = sem("z_ready"), sem("stored")
        filled, act_emptied, dve_emptied = sem("filled"), sem("act_emptied"), sem("dve_emptied")
        stats_ready, rstd_ready, norm_ready = sem("stats_ready"), sem("rstd_ready"), sem("norm_ready")
        one_minus_sq, root_ready, y_ready, gate_sig = sem("one_minus_sq"), sem("root_ready"), sem("y_ready"), sem("gate_sig")
        logits_ready, exps_ready, second_ready, exp2_ready = (sem(n) for n in ("logits_ready", "exps_ready", "second_ready", "exp2_ready"))
        h_ready = sem("h_ready")
        qk_high, qk_mid, qk_low = sem("qk_high"), sem("qk_mid"), sem("qk_low")
        qk_stored = [sem(f"qk_stored{b}") for b in range(NB)]
        products_loaded = [[sem(f"products_loaded{n}{h}") for h in range(GH)] for n in range(2)]
        bias_loaded, varying_ready, v_ready = sem("bias_loaded"), sem("varying_ready"), sem("v_ready")
        ring_filled, ring_emptied, negmax_split = sem("ring_filled"), sem("ring_emptied"), sem("negmax_split")
        negmax_loaded = sem("negmax_loaded")
        scores_filled, exp_done, pv_done, pv_out = sem("scores_filled"), sem("exp_done"), sem("pv_done"), sem("pv_out")
        PER_GROUP = {ring_filled: PER_GROUP_RING, ring_emptied: PER_GROUP_RING, negmax_split: 1, scores_filled: STEPS * GH,
                     exp_done: STEPS * GH, pv_done: STEPS, pv_out: 2, varying_ready: 1, v_ready: 1, negmax_loaded: 16 * NPART,
                     bias_loaded: 16}
        AHEAD = {ring_filled: LEAD, ring_emptied: LEAD, exp_done: 1, pv_done: 1, pv_out: 1}

        def at(G, s, k):
            return G * PER_GROUP[s] + k + AHEAD.get(s, 0)

        def emptied(name):
            engine, k = EMPTYING[name]
            return (act_emptied if engine == "act" else dve_emptied), k

        block = ctx.enter_context(nc.Block())

        def x_tiles(dram, b):
            return dram[b].rearrange("(t p) d -> p t d", p=P)

        def rows_of(m):
            return m.rearrange("(k p) n -> p k n", p=P)

        @block.sync
        def _(sp):
            sp.dma_start(x0[:, 0], x_tiles(x_in, 0)).then_inc(x_loaded[0], 16)
            for dst, src in ((w_inT[:], w["w_inT"]), (w_gateT[:], w["w_gateT"]), (w_aT[:], rows_of(w["w_aT"])),
                             (w_outT[:], rows_of(w["w_outT"]))):
                sp.dma_start(dst, src).then_inc(w_rec, 16)
            for dst, src in ((mgT[:], w["mgT"]), (muT[:], w["muT"]), (mdT[:], rows_of(w["mdT"]))):
                sp.dma_start(dst, src).then_inc(w_mlp, 16)
            for dst, src in ((agT[:], w["agT"]), (gate_b[:], w["gate_b"].broadcast_to([P, NE])), (wiT[:], w["wiT"]),
                             (bT[:], w["bT"]), (woT[:], rows_of(w["woT"]))):
                sp.dma_start(dst, src).then_inc(w_ffn, 16)
            for dst, src in ((wqkvT[:], rows_of(w["wqkvT"])), (gamma[:], w["gamma"].broadcast_to([P, P])),
                             (beta[:], w["beta"].broadcast_to([P, P])), (t_last[:], w["t_last"].broadcast_to([P, GROUPS * GH]))):
                sp.dma_start(dst, src).then_inc(w_att, 16)

            def store_parts(b):
                for k in range(4):
                    which, h = k // 2, k % 2
                    sp.wait_ge(qk_low, 4 * b + k + 1)
                    sp.dma_start(scratch[which, :, b * P:(b + 1) * P, h * HALF:(h + 1) * HALF].rearrange("n p t -> p n t"),
                                 qk_part[:, b, which, :, h * HALF:(h + 1) * HALF]).then_inc(qk_stored[b], 16)
                sp.wait_ge(qk_stored[b], 64)

            def load_products(G, buf):
                for h in range(GH):
                    head = bass.ds(G * GW + h * HD, HD)
                    for i in range(NPART):
                        rows = slice(i * NPART * HD, (i + 1) * NPART * HD)
                        sp.dma_start(qs[rows, buf, h, :], scratch[0, i, head, :].unsqueeze(0).broadcast_to([NPART, HD, S])).then_inc(products_loaded[buf][h], 16)
                        sp.dma_start(ks[rows, buf, h, :], scratch[1, :, head, :]).then_inc(products_loaded[buf][h], 16)

            def load_negmax(G, buf):
                sp.wait_ge(negmax_split, at(G, negmax_split, 1))
                for i in range(NPART):
                    sp.dma_start(qs[STACK + i:STACK + i + 1, buf, :, :].rearrange("o h (t q) -> o (h t) q", q=P),
                                 nm_part[:, buf, i, :]).then_inc(negmax_loaded, 16)

            def load_bias(G):
                sp.dma_start(bias_raw, bass.AP(tensor=tab.tensor, offset=G * (GH * tab.shape[1]),
                                               ap=[[1, P], [tab.shape[1], GH], [1, BIASW]])).then_inc(bias_loaded, 16)

            def group(G, buf, ahead):
                if ahead >= 1:
                    sp.wait_ge(varying_ready, at(G, varying_ready, 1))
                    load_bias(G + 1)
                    load_negmax(G + 1, 1 - buf)
                if ahead >= 2:
                    sp.wait_ge(scores_filled, at(G, scores_filled, STEPS * GH))
                    load_products(G + 2, buf)

            load_bias(0)
            sp.wait_ge(k_ones, 1)
            store_parts(0)
            load_products(0, 0)
            load_products(1, 1)
            store_parts(1)
            load_negmax(0, 0)
            with sp.Fori(0, GROUPS // 2 - 1) as i:
                for n in range(2):
                    group(i * 2 + n, n, 2)
            for n in range(2):
                group(GROUPS - 2 + n, n, 1 - n)
            for b, h in BLOCKS:
                sp.wait_ge(*emptied(f"R1.{b}.{h}"))
                sp.dma_start(x_tiles(out, b)[:, h * TH:(h + 1) * TH, :], x[:, b, h * TH:(h + 1) * TH, :]).then_inc(stored, 16)
            sp.wait_ge(stored, len(BLOCKS) * 16)

        @block.gpsimd
        def _(pool):
            pool.dma_start(x0[:, 1], x_tiles(x_in, 1)).then_inc(x_loaded[1], 16)
            pool.memset(ident[:], 0.0).then_inc(zeroed, 1)
            pool.memset(neghalf[:], -0.5).then_inc(consts, 1)
            pool.memset(ones[:], 1.0).then_inc(consts, 1)
            pool.memset(tiny[:], 1e-8).then_inc(consts, 1)
            pool.memset(one_pair[:], ONE_PAIR).then_inc(consts, 1)
            for e in range(NE):
                pool.memset(rank_of[:, e:e + 1], float(NE - e)).then_inc(consts, 1)
            pool.wait_ge(zeroed, 1)
            pool.affine_select(out=ident[:], in_=ident[:], compare_op=ALU.not_equal, fill=1.0, base=0,
                               pattern=[[-1, P]], channel_multiplier=1).then_inc(consts, 1)
            pool.wait_ge(consts, N_CONSTS)

            def rstds(n, b):
                for h in range(2):
                    pool.wait_ge(stats_ready, 2 * NORM_AT[n, b] + h + 1)
                    pool.tensor_tensor(rstd[:, b, h, :], veps[:, b, h, :], neghalf[:], ALU.pow).then_inc(rstd_ready, 1)

            for b in range(NB):
                rstds(N_REC, b)
            for b in range(NB):
                pool.wait_ge(rstd_ready, 2 * NORM_AT[N_REC, b] + 2)
                for t in range(NT):
                    last = pool.tensor_scalar(z[:, b, t, :], x0[:, b, t, :], mv[:, b, t, 0:1], rstd[:, b, t // TH, t % TH:t % TH + 1],
                                              ALU.subtract, ALU.mult)
                last.then_inc(z_ready, 1)
            pool.memset(vpg, 0.0).then_inc(zeroed, 1)
            pool.wait_ge(zeroed, 2)
            pool.memset(vpg[:, :, :, :, HD:HD + 1], 1.0).then_inc(v_ones, 1)
            pool.wait_ge(v_ones, 1)
            for n in (N_MLP, N_FFN0, N_ATTN):
                for b in range(NB):
                    rstds(n, b)

            def v_copy(G, buf):
                pool.tensor_copy(vpg[:, buf, :, :, 0:HD], v_all[:, bass.ds(G, 1), :, :].rearrange("p o t (h d) -> p (o t) h d", d=HD)).then_inc(v_ready, 1)

            pool.wait_ge(w_att, 16 * 4)
            pool.wait_ge(*emptied("V.0.1"))
            v_copy(0, 0)
            pool.wait_ge(*emptied("V.1.1"))

            def group(G, buf, ahead):
                pool.wait_ge(bias_loaded, at(G, bias_loaded, 16))
                pool.wait_ge(pv_done, at(G, pv_done, 0))
                pool.wait_ge(ring_filled, at(G, ring_filled, 0))
                pool.tensor_tensor(pause[:], neghalf[:], neghalf[:], ALU.add)
                pool.tensor_tensor(varying, bias_raw[:, :, ::-1], t_last[:, bass.ds(G * GH, GH)].unsqueeze(2).broadcast_to([P, GH, BIASW]),
                                   ALU.subtract).then_inc(varying_ready, 1)
                if ahead:
                    v_copy(G + 1, 1 - buf)
                pool.drain()

            with pool.Fori(0, GROUPS // 2 - 1) as i:
                for n in range(2):
                    group(i * 2 + n, n, True)
            for n in range(2):
                group(GROUPS - 2 + n, n, n == 0)
            for b in range(NB):
                rstds(N_OUT, b)
                rstds(N_FFN1, b)

        @block.scalar
        def _(act):
            for dst, src in ((ln1_w[:], w["ln1_w"]), (a_param[:], w["a_param"]), (ln2_w[:], w["ln2_w"]), (bi[:], w["bi"]), (bo[:], w["bo"])):
                act.dma_start(dst, src).then_inc(w_small, 16)

            def take(name, dst, func=ACT.Identity, signal=None, **kw):
                act.wait_ge(filled, INDEX[name] + 1)
                act.activation(dst, banks[:, BANK[name], :], func, **kw).then_inc(signal or act_emptied, 1)

            def half(tile, h):
                return tile[:, h * HALF:(h + 1) * HALF]

            def ffn(f):
                for b, h in BLOCKS:
                    take(f"T{f}.{b}.{h}", half(hT[:, b], h))
                for b in range(NB):
                    act.wait_ge(logits_ready, NB * f + b + 1)
                    act.activation(ex[:, b], ls[:, b], ACT.Exp).then_inc(exps_ready, 1)
                    act.wait_ge(second_ready, NB * f + b + 1)
                    act.activation(e2[:, b], m2[:, b], ACT.Exp).then_inc(exp2_ready, 1)
                    if b == 0:
                        expand(f, 0)
                for q in range(len(BLOCKS) + 1):
                    if 1 <= q < 4:
                        expand(f, q)
                    if q >= 1:
                        b, h = BLOCKS[q - 1]
                        take(f"O{f}.{b}.{h}", half(oT[:, b], h), bias=bo2[:])

            def expand(f, q):
                b, h = BLOCKS[q]
                h0, _, _, _, umT = moe[b]
                for k in range(2):
                    take(f"X{f}.{b}.{h}.{k}", half(umT[:, k, :], h))
                for c in range(FC):
                    if h:
                        act.wait_ge(h_ready, (f * len(BLOCKS) + q - 1) * FC + c + 1)
                    take(f"HA{f}.{b}.{h}.{c}", h0[:, c, :], ACT.Relu, bias=bi[:, c:c + 1])

            act.wait_ge(consts, N_CONSTS)
            act.activation(k_words[64:96], one_pair[64:96].broadcast_to([32, 2 * GH * S // 2]), ACT.Copy).then_inc(k_ones, 1)
            act.wait_ge(w_small, 16 * 5)
            for b in range(NB):
                xinT, gT, aT, sT, _ = rec[b]
                for h in range(2):
                    take(f"Trec.{b}.{h}", half(hT[:, b], h), scale=ln1_w[:])
                for h in range(2):
                    for c in range(REC):
                        take(f"XI.{b}.{h}.{c}", half(xinT[:, c, :], h))
                for h in range(2):
                    for c in range(REC):
                        take(f"G.{b}.{h}.{c}", half(gT[:, c, :], h), ACT.Sigmoid)
                for c in range(REC):
                    for h in range(2):
                        take(f"A.{b}.{h}.{c}", half(aT[:, c, :], h), ACT.Sigmoid, bias=a_param[:, c:c + 1])
                for c in range(REC):
                    act.wait_ge(one_minus_sq, REC * b + c + 1)
                    act.activation(sT[:, c, :], sT[:, c, :], ACT.Sqrt, bias=tiny[:]).then_inc(root_ready, 1)
            for b, h in BLOCKS:
                take(f"WO.{b}.{h}", half(oT[:, b], h))
            for b, h in BLOCKS:
                take(f"Tmlp.{b}.{h}", half(hT[:, b], h), scale=ln2_w[:])
            for q in range(len(BLOCKS) + 1):
                if q < 4:
                    b, h = BLOCKS[q]
                    sg = mlp[b][0]
                    for c in range(FC):
                        k = h * FC + c
                        if k >= 2:
                            act.wait_ge(*emptied(f"MG.{b}.{(k - 2) // FC}.{(k - 2) % FC}"))
                        take(f"MG.{b}.{h}.{c}", sg[:, k % 2, :], ACT.Sigmoid, signal=gate_sig)
                if q >= 1:
                    b, h = BLOCKS[q - 1]
                    take(f"MD.{b}.{h}", half(oT[:, b], h))
            act.wait_ge(bo2_ready, 1)
            ffn(0)

            def part_of(b, k, i):
                return half(qk_part[:, b, k // 2, i, :], k % 2)

            def mid(b, k):
                act.wait_ge(*emptied(f"QK.{b}.{k // 2}.{k % 2}"))
                act.activation(part_of(b, k, 1), half(qk_rest[:, b, k // 2, :], k % 2), ACT.Copy).then_inc(qk_mid, 1)

            for b in range(NB):
                for h in range(2):
                    take(f"Tatt.{b}.{h}", half(hT[:, b], h))
                for k in range(4):
                    take(f"QK.{b}.{k // 2}.{k % 2}", part_of(b, k, 0), ACT.Copy, signal=qk_high)
                    if k:
                        mid(b, k - 1)
                mid(b, 3)

            def group(G):
                def take_pv(q):
                    act.wait_ge(pv_done, at(G, pv_done, NT * (q + 1)))
                    act.activation(half(pvT, q), pv_bank, ACT.Copy).then_inc(pv_out, 1)

                for s in range(STEPS):
                    if s == 0:
                        act.wait_ge(pv_done, at(G, pv_done, 0))
                    elif s >= 2:
                        act.wait_ge(pv_done, at(G, pv_done, s - 1))
                    for h in range(GH):
                        n = s * GH + h
                        act.wait_ge(scores_filled, at(G, scores_filled, n + 1))
                        act.activation(probs[:, s % 2, h, :], score_bank(n), ACT.Exp, scale=SCALE).then_inc(exp_done, 1)
                    if s == NT:
                        act.wait_ge(ring_filled, at(G, ring_filled, 0))
                        take_pv(0)
                take_pv(1)

            act.nop().then_inc(exp_done, AHEAD[exp_done])
            act.nop().then_inc(pv_out, AHEAD[pv_out])
            with act.Fori(0, GROUPS // 2 - 1) as i:
                for n in range(2):
                    group(i * 2 + n)
            for G in range(GROUPS - 2, GROUPS):
                group(G)
            ffn(1)

        @block.vector
        def _(dve):
            def bank(name, width=HALF):
                return banks[:, BANK[name], 0:width]

            def wait_filled(name):
                dve.wait_ge(filled, INDEX[name] + 1)

            def tiles(h):
                return slice(h * TH, (h + 1) * TH)

            def tile_of(src, b, t):
                if src is o_tok:
                    return o_tok[:, b * NG:(b + 1) * NG, t, :]
                return src[:, b, t, :]

            def stats_half(n, b, src, h):
                for t in range(h * TH, (h + 1) * TH):
                    dve.bn_stats(stats[:, b, t, :], tile_of(src, b, t))
                dve.drain()
                for t in range(h * TH, (h + 1) * TH):
                    dve.bn_aggr(mv[:, b, t, :], stats[:, b, t, :])
                dve.drain()
                mean, var = mv[:, b, tiles(h), 0], mv[:, b, tiles(h), 1]
                if n == N_MLP:
                    dve.tensor_tensor(msq[:, b, tiles(h)], mean, mean, ALU.mult)
                    dve.drain()
                    dve.scalar_tensor_tensor(out=veps[:, b, h, 0:TH], in0=var, scalar=RMS_EPS, in1=msq[:, b, tiles(h)],
                                             op0=ALU.add, op1=ALU.add).then_inc(stats_ready, 1)
                elif n == N_REC:
                    dve.tensor_scalar(veps[:, b, h, TH:2 * TH], var, 1.0 + RMS_EPS, RMS_EPS * LN_EPS, ALU.mult, ALU.add)
                    dve.drain()
                    dve.tensor_scalar(veps[:, b, h, 0:TH], var, LN_EPS, None, ALU.add).then_inc(stats_ready, 1)
                else:
                    dve.tensor_scalar(veps[:, b, h, 0:TH], var, LN_EPS, None, ALU.add).then_inc(stats_ready, 1)

            def normed_half(n, b, src, h):
                dve.wait_ge(rstd_ready, 2 * NORM_AT[n, b] + h + 1)
                for t in range(h * TH, (h + 1) * TH):
                    r = rstd[:, b, h, TH + t % TH:TH + t % TH + 1] if n == N_REC else rstd[:, b, h, t % TH:t % TH + 1]
                    dst = tile_of(nt, b, t) if src is not o_tok else nt[:, b, t, :].rearrange("p (g c) -> p g c", g=NG)
                    if n == N_MLP:
                        last = dve.tensor_scalar(dst, tile_of(src, b, t), r, None, ALU.mult)
                    else:
                        last = dve.tensor_scalar(dst, tile_of(src, b, t), mv[:, b, t, 0:1], r, ALU.subtract, ALU.mult)
                if n != N_OUT:
                    last.then_inc(norm_ready, 1)

            def norm(n, b, src):
                dve.drain()
                for h in range(2):
                    stats_half(n, b, src, h)
                for h in range(2):
                    normed_half(n, b, src, h)

            def per_tile(v):
                return v.unsqueeze(2).broadcast_to([P, NT, NE])

            ranks = rank_of[:].unsqueeze(1).broadcast_to([P, NT, NE])

            def first_of(b, scores, top, k, pick):
                dve.tensor_tensor(key[:, b], scores[:, b], top, ALU.is_equal)
                dve.drain()
                dve.tensor_tensor(key[:, b], key[:, b], ranks, ALU.mult)
                dve.drain()
                dve.tensor_reduce(k[:, b], key[:, b], axis=AXX, op=ALU.max)
                dve.drain()
                dve.tensor_tensor(pick[:, b], ranks, per_tile(k[:, b]), ALU.is_equal)
                dve.drain()

            def route(f, b):
                for j in range(NT // 2):
                    wait_filled(f"U{f}.{b}.{j}")
                    u = bank(f"U{f}.{b}.{j}", 2 * UW).rearrange("p (t c) -> p t c", c=UW)
                    dve.tensor_tensor(lg[:, b, 2 * j:2 * j + 2, :], u[:, :, P:UW], gate_b[:].unsqueeze(1).broadcast_to([P, 2, NE]), ALU.add)
                dve.drain()
                dve.tensor_reduce(m1[:, b], lg[:, b], axis=AXX, op=ALU.max)
                dve.drain()
                dve.tensor_tensor(ls[:, b], lg[:, b], per_tile(m1[:, b]), ALU.subtract)
                dve.drain()
                dve.tensor_scalar(ls[:, b], ls[:, b], UNDERFLOW, None, ALU.max).then_inc(logits_ready, 1)
                dve.drain()
                first_of(b, ls, per_tile(zero_t[:]), k1, pick0)
                dve.scalar_tensor_tensor(out=ls2[:, b].rearrange("p t e -> p (t e)"), in0=pick0[:, b].rearrange("p t e -> p (t e)"), scalar=-1e30,
                                         in1=ls[:, b].rearrange("p t e -> p (t e)"), op0=ALU.mult, op1=ALU.add)
                dve.drain()
                dve.tensor_reduce(m2[:, b], ls2[:, b], axis=AXX, op=ALU.max).then_inc(second_ready, 1)
                dve.drain()
                first_of(b, ls2, per_tile(m2[:, b]), k2, pick1)
                dve.tensor_tensor(pickd[:, b], pick1[:, b], pick0[:, b], ALU.subtract)
                dve.drain()
                um = moe[b][3]
                for j in range(NT // 2):
                    u = bank(f"U{f}.{b}.{j}", 2 * UW).rearrange("p (t c) -> p t c", c=UW)[:, :, 0:P].rearrange("p t (e r) -> p t e r", r=RANK)
                    for k, pick in enumerate((pick0, pickd)):
                        last = dve.tensor_tensor(um[:, k, 2 * j:2 * j + 2, :].rearrange("p t (e r) -> p t e r", r=RANK), u,
                                                 pick[:, b, 2 * j:2 * j + 2, :].unsqueeze(3).broadcast_to([P, 2, NE, RANK]), ALU.mult)
                    last.then_inc(dve_emptied, 1)
                dve.wait_ge(exps_ready, NB * f + b + 1)
                dve.tensor_reduce(esum[:, b], ex[:, b], axis=AXX, op=ALU.add)
                dve.drain()
                dve.reciprocal(ersum[:, b], esum[:, b])
                dve.drain()
                dve.wait_ge(exp2_ready, NB * f + b + 1)
                dve.scalar_tensor_tensor(out=val[:, b], in0=e2[:, b], scalar=1.0, in1=ersum[:, b], op0=ALU.add, op1=ALU.mult)

            def sums(f, q):
                b, h = BLOCKS[q]
                h0, h1, hs, _, _ = moe[b]
                for c in range(FC):
                    name = f"HB{f}.{b}.{h}.{c}"
                    wait_filled(name)
                    dve.tensor_scalar(h1[:, c % 2, :], bank(name), bi[:, c:c + 1], 0.0, ALU.add, ALU.max).then_inc(dve_emptied, 1)
                    dve.wait_ge(*emptied(name))
                    dve.tensor_tensor(hs[:, c, h * HALF:(h + 1) * HALF], h1[:, c % 2, :], h0[:, c, :], ALU.add).then_inc(h_ready, 1)

            def add_ffn(f, q):
                b, h = BLOCKS[q]
                name = f"R{f}.{b}.{h}"
                wait_filled(name)
                for t in range(h * TH, (h + 1) * TH):
                    last = dve.scalar_tensor_tensor(out=x[:, b, t, :], in0=bank(name)[:, (t % TH) * P:(t % TH + 1) * P], scalar=val[:, b, t:t + 1],
                                                    in1=x[:, b, t, :], op0=ALU.mult, op1=ALU.add)
                last.then_inc(dve_emptied, 1)

            def ffn(f, after):
                for b in range(NB):
                    route(f, b)
                    if b == 0:
                        sums(f, 0)
                for q in range(1, len(BLOCKS) + 2):
                    if q < 4:
                        sums(f, q)
                    if q >= 2:
                        add_ffn(f, q - 2)
                        if q % 2 and after:
                            after((q - 2) // 2)

            dve.memset(zero_t[:], 0.0)
            for b in range(NB):
                dve.wait_ge(x_loaded[b], 16)
                norm(N_REC, b, x0)
            dve.wait_ge(w_small, 16 * 5)
            dve.tensor_scalar(bo2[:], bo[:], 2.0, None, ALU.mult).then_inc(bo2_ready, 1)
            for b in range(NB):
                xinT, gT, aT, sT, yT = rec[b]
                for c in range(REC):
                    dve.wait_ge(*emptied(f"A.{b}.1.{c}"))
                    dve.tensor_tensor(sT[:, c, :], aT[:, c, :], aT[:, c, :], ALU.mult)
                    dve.drain()
                    dve.tensor_scalar(sT[:, c, :], sT[:, c, :], -1.0, 1.0, ALU.mult, ALU.add).then_inc(one_minus_sq, 1)
                for c in range(REC):
                    dve.wait_ge(root_ready, REC * b + c + 1)
                    dve.tensor_tensor(sT[:, c, :], sT[:, c, :], xinT[:, c, :], ALU.mult)
                    dve.drain()
                    dve.tensor_tensor_scan(yT[:, c, :], aT[:, c, :], sT[:, c, :], 0.0, ALU.mult, ALU.add)
                    dve.drain()
                    dve.tensor_tensor(yT[:, c, :], yT[:, c, :], gT[:, c, :], ALU.mult).then_inc(y_ready, 1)
            for b in range(NB):
                dve.wait_ge(z_ready, b + 1)
                for h in range(2):
                    wait_filled(f"Rrec.{b}.{h}")
                    dve.tensor_tensor(x1[:, b, tiles(h), :], z[:, b, tiles(h), :], bank(f"Rrec.{b}.{h}").rearrange("p (t d) -> p t d", d=P), ALU.add).then_inc(dve_emptied, 1)
                    dve.drain()
                    stats_half(N_MLP, b, x1, h)
                for h in range(2):
                    normed_half(N_MLP, b, x1, h)
                dve.tensor_tensor(x[:, b], x0[:, b], x1[:, b], ALU.add)
            dve.drain()
            dve.wait_ge(w_ffn, 16 * 5)
            for q in range(len(BLOCKS) + 2):
                if q < 4:
                    b, h = BLOCKS[q]
                    sg, sgu, m_T = mlp[b]
                    for c in range(FC):
                        k = h * FC + c
                        dve.wait_ge(gate_sig, q * FC + c + 1)
                        dve.tensor_tensor(sgu[:, k % 2, :], sg[:, k % 2, :], bank(f"MG.{b}.{h}.{c}"), ALU.mult).then_inc(dve_emptied, 1)
                        wait_filled(f"MU.{b}.{h}.{c}")
                        dve.wait_ge(*emptied(f"MG.{b}.{h}.{c}"))
                        dve.tensor_tensor(m_T[:, c, h * HALF:(h + 1) * HALF], sgu[:, k % 2, :], bank(f"MU.{b}.{h}.{c}"), ALU.mult).then_inc(dve_emptied, 1)
                if q >= 2:
                    b, h = BLOCKS[q - 2]
                    wait_filled(f"Rmlp.{b}.{h}")
                    dve.tensor_tensor(x[:, b, tiles(h), :], x[:, b, tiles(h), :], bank(f"Rmlp.{b}.{h}").rearrange("p (t d) -> p t d", d=P), ALU.add).then_inc(dve_emptied, 1)
                    if h:
                        norm(N_FFN0, b, x)
            ffn(0, lambda b: norm(N_ATTN, b, x))

            def part_of(b, k, i):
                return qk_part[:, b, k // 2, i, (k % 2) * HALF:(k % 2 + 1) * HALF]

            def rest_of(b, k):
                return qk_rest[:, b, k // 2, (k % 2) * HALF:(k % 2 + 1) * HALF]

            def low(b, k):
                dve.wait_ge(qk_mid, 4 * b + k + 1)
                dve.tensor_tensor(part_of(b, k, 2), rest_of(b, k), part_of(b, k, 1), ALU.subtract).then_inc(qk_low, 1)

            for b in range(NB):
                for k in range(4):
                    dve.wait_ge(qk_high, 4 * b + k + 1)
                    dve.tensor_tensor(rest_of(b, k), bank(f"QK.{b}.{k // 2}.{k % 2}"), part_of(b, k, 0), ALU.subtract).then_inc(dve_emptied, 1)
                    if k:
                        low(b, k - 1)
                low(b, 3)
            dve.wait_ge(w_att, 16 * 4)
            for b in range(NB):
                for h in range(2):
                    wait_filled(f"V.{b}.{h}")
                    dve.tensor_copy(v_all[:, b * NG:(b + 1) * NG, tiles(h), :], bank(f"V.{b}.{h}").rearrange("p (t g c) -> p g t c", g=NG, c=GW)).then_inc(dve_emptied, 1)
                wait_filled(f"CS.{b}")
                dve.tensor_tensor(cs[:, b].rearrange("p (h d) -> p h d", d=HD), bank(f"CS.{b}", P).rearrange("p (h d) -> p h d", d=HD),
                                  t_last[:, b * NH:(b + 1) * NH].unsqueeze(2).broadcast_to([P, NH, HD]), ALU.mult).then_inc(dve_emptied, 1)

            def max_item(slot, buf, k):
                return dve.tensor_reduce(negmax[:, buf, k:k + 1], slot.rearrange("p a b -> p (a b)"), axis=AXX, op=ALU.max, negate=True)

            def split_negmax(slot, buf):
                rows = slot[0:GH * NT, 0, 0:P]
                dve.tensor_copy(nm_part[:, buf, 0, :], rows)
                dve.drain()
                dve.tensor_tensor(nm_rest[:], rows, nm_part[:, buf, 0, :], ALU.subtract).then_inc(ring_emptied, 1)
                dve.drain()
                dve.tensor_copy(nm_part[:, buf, 1, :], nm_rest[:])
                dve.drain()
                dve.tensor_tensor(nm_part[:, buf, 2, :], nm_rest[:], nm_part[:, buf, 1, :], ALU.subtract).then_inc(negmax_split, 1)

            for k in range(LEAD):
                dve.wait_ge(ring_filled, k + 1)
                if k < MAXES:
                    max_item(slot_of(k), 0, k).then_inc(ring_emptied, 1)
                else:
                    split_negmax(slot_of(k), 0)

            def group(G, buf, ahead):
                first = 0 if ahead else BIAS
                for k in range(first, PER_GROUP_RING):
                    slot = slot_of(LEAD + k - first)
                    dve.wait_ge(ring_filled, at(G, ring_filled, k - first + 1))
                    if k < MAXES:
                        max_item(slot, 1 - buf, k).then_inc(ring_emptied, 1)
                    elif k == MTR:
                        split_negmax(slot, 1 - buf)
                    elif k == BIAS:
                        dve.tensor_copy(biasT, slot[:, 0, :]).then_inc(ring_emptied, 1)
                    elif k == BTR:
                        dve.tensor_copy(bias_tok[:], slot[:, 0, :].rearrange("p (t g v) -> p t g v", g=GH, v=VW)[:, :, :, 0:HD]).then_inc(ring_emptied, 1)
                    else:
                        o = slot.rearrange("p a (t g v) -> p (a t) g v", g=GH, v=VW)
                        dst = o_tok[:, bass.ds(G, 1), :, :].rearrange("p o t (g d) -> p (o t) g d", d=HD)
                        dve.reciprocal(rl[:], o[:, :, :, HD])
                        dve.drain()
                        dve.tensor_tensor(dst, o[:, :, :, 0:HD], rl[:].unsqueeze(3).broadcast_to([P, NT, GH, HD]), ALU.mult).then_inc(ring_emptied, 1)
                        dve.drain()
                        dve.tensor_tensor(dst[:, 0:TH], dst[:, 0:TH], bias_tok[:], ALU.add)
                        dve.drain()

            def attended(b):
                o = o_tok[:, b * NG:(b + 1) * NG, :, :]
                dve.tensor_tensor(o, o, cs[:, b].rearrange("p (g c) -> p g c", g=NG).unsqueeze(2).broadcast_to([P, NG, NT, GW]), ALU.add)
                norm(N_OUT, b, o_tok)
                for op, tile in ((ALU.mult, gamma), (ALU.add, beta)):
                    dve.drain()
                    dve.tensor_tensor(nt[:, b], nt[:, b], tile[:].unsqueeze(1).broadcast_to([P, NT, P]), op)
                dve.drain()
                dve.tensor_tensor(x[:, b], x[:, b], nt[:, b], ALU.add)
                norm(N_FFN1, b, x)

            with dve.Fori(0, GROUPS // 2 - 1) as i:
                for n in range(2):
                    group(i * 2 + n, n, True)
            group(GROUPS - 2, 0, True)
            attended(0)
            group(GROUPS - 1, 1, False)
            attended(1)
            ffn(1, None)

        @block.tensor
        def _(pe):
            def begin(name):
                if BEFORE[name]:
                    pe.wait_ge(*emptied(BEFORE[name]))

            def dense(name, terms):
                begin(name)
                for i, (lhsT, rhs) in enumerate(terms):
                    last = pe.matmul(banks[:, BANK[name], :], lhsT, rhs, start=i == 0, stop=i == len(terms) - 1)
                last.then_inc(filled, 1)

            def flip(name, blocks):
                begin(name)
                for i, src in enumerate(blocks):
                    last = pe.transpose(banks[:, BANK[name], i * P:(i + 1) * P], src, ident[:])
                last.then_inc(filled, 1)

            def half(tile, h):
                return tile[:, h * HALF:(h + 1) * HALF]

            def chunk(tile, c):
                return tile[:, c * P:(c + 1) * P]

            def flip_norm(n, b, prefix):
                for h in range(2):
                    pe.wait_ge(norm_ready, 2 * FLIPPED_AT[n, b] + h + 1)
                    flip(f"{prefix}.{b}.{h}", [nt[:, b, h * TH + i, :] for i in range(TH)])

            def back(src_job, job, b, h):
                pe.wait_ge(*emptied(f"{src_job}.{b}.{h}"))
                flip(f"{job}.{b}.{h}", [chunk(oT[:, b], h * TH + i) for i in range(TH)])

            def ffn(f):
                def logits(b):
                    for j in range(NT // 2):
                        name = f"U{f}.{b}.{j}"
                        pe.wait_ge(*emptied(f"T{f}.{b}.{j // 2}"))
                        begin(name)
                        for i in range(2):
                            last = pe.matmul(banks[:, BANK[name], i * UW:(i + 1) * UW], chunk(hT[:, b], 2 * j + i), agT[:], start=True, stop=True)
                        last.then_inc(filled, 1)

                flip_norm((N_FFN0, N_FFN1)[f], 0, f"T{f}")
                logits(0)
                flip_norm((N_FFN0, N_FFN1)[f], 1, f"T{f}")

                def base(b, h, c):
                    begin(f"HA{f}.{b}.{h}.{c}")
                    pe.matmul(banks[:, BANK[f"HA{f}.{b}.{h}.{c}"], :], chunk(wiT, c), half(hT[:, b], h), start=True, stop=False, skip_group_check=True)

                def lora(name, b, h, c, k):
                    pe.matmul(banks[:, BANK[name], :], chunk(bT, c), half(moe[b][4][:, k, :], h), start=False, stop=k == 1, skip_group_check=True).then_inc(filled, 1)

                for q in range(len(BLOCKS) + 2):
                    if q < 4:
                        b, h = BLOCKS[q]
                        if h == 0:
                            pe.wait_ge(*emptied(f"U{f}.{b}.3"))
                        for k in range(2):
                            flip(f"X{f}.{b}.{h}.{k}", [moe[b][3][:, k, h * TH + i, :] for i in range(TH)])
                        base(b, h, 0)
                        base(b, h, 1)
                        pe.wait_ge(*emptied(f"X{f}.{b}.{h}.1"))
                        for c in range(FC):
                            if c >= 2:
                                base(b, h, c)
                            lora(f"HA{f}.{b}.{h}.{c}", b, h, c, 0)
                        for c in range(FC):
                            pe.wait_ge(*emptied(f"HA{f}.{b}.{h}.{c}"))
                            lora(f"HB{f}.{b}.{h}.{c}", b, h, c, 1)
                        if q == 0:
                            logits(1)
                    if 1 <= q < 5:
                        b, h = BLOCKS[q - 1]
                        pe.wait_ge(h_ready, (f * len(BLOCKS) + q) * FC)
                        dense(f"O{f}.{b}.{h}", [(woT[:, c, :], half(moe[b][2][:, c, :], h)) for c in range(FC)])
                    if q >= 2:
                        back(f"O{f}", f"R{f}", *BLOCKS[q - 2])

            pe.wait_ge(consts, N_CONSTS)
            for b in range(NB):
                xinT = rec[b][0]
                flip_norm(N_REC, b, "Trec")
                pe.wait_ge(w_rec, 16 * 4)
                for h in range(2):
                    pe.wait_ge(*emptied(f"Trec.{b}.{h}"))
                    for c in range(REC):
                        dense(f"XI.{b}.{h}.{c}", [(chunk(w_inT, c), half(hT[:, b], h))])
                for h in range(2):
                    for c in range(REC):
                        dense(f"G.{b}.{h}.{c}", [(chunk(w_gateT, c), half(hT[:, b], h))])
                for c in range(REC):
                    for h in range(2):
                        pe.wait_ge(*emptied(f"XI.{b}.{h}.1"))
                        dense(f"A.{b}.{h}.{c}", [(chunk(w_aT[:, k, :], c), half(xinT[:, k, :], h)) for k in range(REC)])
            for b in range(NB):
                pe.wait_ge(y_ready, REC * (b + 1))
                for h in range(2):
                    dense(f"WO.{b}.{h}", [(w_outT[:, k, :], half(rec[b][4][:, k, :], h)) for k in range(REC)])
                for h in range(2):
                    back("WO", "Rrec", b, h)
            for b in range(NB):
                flip_norm(N_MLP, b, "Tmlp")
            pe.wait_ge(w_mlp, 16 * 3)
            for q in range(len(BLOCKS) + 2):
                if q < 4:
                    b, h = BLOCKS[q]
                    pe.wait_ge(*emptied(f"Tmlp.{b}.{h}"))
                    for c in range(FC):
                        dense(f"MG.{b}.{h}.{c}", [(chunk(mgT, c), half(hT[:, b], h))])
                        dense(f"MU.{b}.{h}.{c}", [(chunk(muT, c), half(hT[:, b], h))])
                if 1 <= q < 5:
                    b, h = BLOCKS[q - 1]
                    pe.wait_ge(*emptied(f"MU.{b}.{h}.{FC - 1}"))
                    dense(f"MD.{b}.{h}", [(mdT[:, c, :], half(mlp[b][2][:, c, :], h)) for c in range(FC)])
                if q >= 2:
                    back("MD", "Rmlp", *BLOCKS[q - 2])
            pe.wait_ge(w_ffn, 16 * 5)
            ffn(0)
            pe.wait_ge(w_att, 16 * 4)
            for b in range(NB):
                flip_norm(N_ATTN, b, "Tatt")
                for which in range(2):
                    for h in range(2):
                        pe.wait_ge(*emptied(f"Tatt.{b}.{h}"))
                        dense(f"QK.{b}.{which}.{h}", [(wqkvT[:, which, :], half(hT[:, b], h))])
            for b in range(NB):
                for h in range(2):
                    name = f"V.{b}.{h}"
                    begin(name)
                    for i in range(TH):
                        last = pe.matmul(banks[:, BANK[name], i * P:(i + 1) * P], chunk(hT[:, b], h * TH + i), wqkvT[:, 2, :], start=True, stop=True)
                    last.then_inc(filled, 1)
                begin(f"CS.{b}")
                pe.wait_ge(*emptied(f"V.{b}.1"))
                for t in range(NT):
                    last = pe.matmul(banks[:, BANK[f"CS.{b}"], 0:P], ones[:], v_all[:, b * NG:(b + 1) * NG, t, :], start=t == 0, stop=t == NT - 1)
                last.then_inc(filled, 1)
            pe.wait_ge(*emptied("CS.1"))

            def max_item(slot, buf, k):
                h, t = k // NT, k % NT
                for half_ in range(2):
                    last = pe.matmul(slot[:, half_, :], qs[0:STACK, buf, h, t * P:(t + 1) * P], ks[0:STACK, buf, h, half_ * HALF:(half_ + 1) * HALF],
                                     start=True, stop=True)
                last.then_inc(ring_filled, 1)

            def products(G, buf, k):
                if k % NT == 0:
                    pe.wait_ge(products_loaded[buf][k // NT], G * (16 * NPART) + (16 * 2 * NPART - buf * 16 * NPART))

            for k in range(LEAD):
                if k >= 2:
                    pe.wait_ge(ring_emptied, k - 1)
                if k < MAXES:
                    products(0, 0, k)
                    max_item(slot_of(k), 0, k)
                else:
                    pe.wait_ge(ring_emptied, MAXES)
                    pe.transpose(slot_of(k)[0:GH * NT, 0, 0:P], negmax[:, 0, :], ident[:]).then_inc(ring_filled, 1)

            def group(G, buf, ahead):
                count = [0]

                def slot():
                    k = count[0]
                    count[0] += 1
                    pe.wait_ge(ring_emptied, at(G, ring_emptied, k - 1))
                    return slot_of(LEAD + k)

                def scores(s, h):
                    n = s * GH + h
                    if n == 0:
                        pe.wait_ge(negmax_loaded, at(G, negmax_loaded, 16 * NPART))
                        pe.wait_ge(exp_done, at(G, exp_done, 0))
                    elif n >= 3:
                        pe.wait_ge(exp_done, at(G, exp_done, n - 2))
                    t, q = s % NT, s // NT
                    pe.matmul(score_bank(n), ks[0:DEPTH, buf, h, t * P:(t + 1) * P], qs[0:DEPTH, buf, h, q * HALF:(q + 1) * HALF],
                              start=True, stop=True).then_inc(scores_filled, 1)

                def weigh(s):
                    t, q = s % NT, s // NT
                    pe.wait_ge(exp_done, at(G, exp_done, (s + 1) * GH))
                    if t == 0:
                        if q == 0:
                            pe.wait_ge(v_ready, at(G, v_ready, 1))
                        pe.wait_ge(pv_out, at(G, pv_out, q))
                    for h in range(GH):
                        last = pe.matmul(pv_bank[32 * h:32 * h + VW, :], vpg[:, buf, t, h, :], probs[:, s % 2, h, :],
                                         start=t == 0, stop=t == NT - 1)
                    last.then_inc(pv_done, 1)

                for s in range(STEPS):
                    scores(s, 0)
                    if ahead:
                        products(G + 1, 1 - buf, 2 * s)
                        max_item(slot(), 1 - buf, 2 * s)
                    scores(s, 1)
                    if s:
                        weigh(s - 1)
                    scores(s, 2)
                    if ahead:
                        max_item(slot(), 1 - buf, 2 * s + 1)
                    scores(s, 3)
                if ahead:
                    place = slot()
                    pe.wait_ge(ring_emptied, at(G, ring_emptied, MAXES))
                    pe.transpose(place[0:GH * NT, 0, 0:P], negmax[:, 1 - buf, :], ident[:]).then_inc(ring_filled, 1)
                place = slot()
                pe.wait_ge(varying_ready, at(G, varying_ready, 1))
                for t in range(NT - 1, TH - 1, -1):
                    skip = (NT - 1 - t) * P
                    for h in range(GH):
                        last = pe.matmul(place[32 * h:32 * h + VW, 0, 0:BIASW - skip], vpg[:, buf, t, h, :], varying[:, h, skip:BIASW],
                                         start=t == NT - 1, stop=t == TH)
                last.then_inc(ring_filled, 1)
                weigh(STEPS - 1)
                place = slot()
                pe.wait_ge(ring_emptied, at(G, ring_emptied, count[0] - 1))
                for t in range(TH):
                    last = pe.transpose(place[:, 0, t * P:(t + 1) * P], chunk(biasT, t), ident[:])
                last.then_inc(ring_filled, 1)
                place = slot()
                pe.wait_ge(pv_out, at(G, pv_out, 2))
                for t in range(NT):
                    last = pe.transpose(place[:, t // TH, (t % TH) * P:(t % TH + 1) * P], chunk(pvT, t), ident[:])
                last.then_inc(ring_filled, 1)

            pe.nop().then_inc(pv_done, AHEAD[pv_done])
            with pe.Fori(0, GROUPS // 2 - 1) as i:
                for n in range(2):
                    group(i * 2 + n, n, True)
            for n in range(2):
                group(GROUPS - 2 + n, n, n == 0)
            pe.wait_ge(ring_emptied, at(GROUPS - 1, ring_emptied, LAST_RING))
            ffn(1)
    return nc


def kernel(**inputs):
    import concourse.bacc as bacc
    from concourse.bass_utils import run_bass_kernel_spmd

    a = {k[3:]: np.asarray(v) for k, v in inputs.items()}

    def col(v, n=1):
        return v.reshape(n, P).T

    clipped = np.minimum(np.arange(P - 1 + BIASW), LAST)
    laid = {
        "x": a["attn_a_x"], "ln1_w": col(a["attn_a_ln1_w"]), "ln2_w": col(a["attn_a_ln2_w"]),
        "w_inT": a["attn_a_w_in"].T, "w_gateT": a["attn_a_w_gate"].T, "w_aT": a["attn_a_w_a"].T, "w_outT": a["attn_a_w_out"].T,
        "a_param": col(a["attn_a_a_param"], REC), "mgT": a["attn_a_w_mlp_gate"].T, "muT": a["attn_a_w_mlp_up"].T,
        "mdT": a["attn_a_w_mlp_down"].T,
        "wqkvT": np.concatenate([a["attn_b_Wq"].T, a["attn_b_Wk"].T, a["attn_b_Wv"].T]),
        "tab": np.tile(a["attn_b_rel_bias_table"].T[:, clipped[::-1]], (NB, 1)),
        "t_last": np.tile(a["attn_b_rel_bias_table"][LAST:LAST + 1], (1, NB)),
        "gamma": a["attn_b_ln_gamma"].reshape(1, P), "beta": a["attn_b_ln_beta"].reshape(1, P),
        "wiT": a["ffn_wi"].T, "bi": col(a["ffn_bi"], FC), "woT": a["ffn_wo"].T, "bo": col(a["ffn_bo"]),
        "agT": np.concatenate([a["ffn_lora_A"].reshape(P, P), a["ffn_gate_w"]]).T,
        "bT": a["ffn_lora_B"].transpose(0, 2, 1).reshape(P, FC * P), "gate_b": a["ffn_gate_b"].reshape(1, NE),
    }
    nc = bacc.Bacc("TRN2", target_bir_lowering=False, num_devices=1)
    arrays, aps = {}, {}
    for name, v in laid.items():
        arrays[f"in_{name}"] = np.ascontiguousarray(v)
        aps[name] = nc.dram_tensor(f"in_{name}", v.shape, FP32, kind="ExternalInput").ap()
    out = nc.dram_tensor("out", (NB, S, P), FP32, kind="ExternalOutput").ap()
    build(nc, aps.pop("x"), out, aps, aps.pop("tab"))
    return run_bass_kernel_spmd(nc, [arrays], core_ids=[0]).results[0]["out"]
```

```python
import numpy as np
import concourse.bass as bass
from concourse import mybir
from contextlib import ExitStack

FP32 = mybir.dt.float32
BF16 = mybir.dt.bfloat16
ALU = mybir.AluOpType
ACT = mybir.ActivationFunctionType
AXX = mybir.AxisListType.X

P = 128
NB = 2
S = 1024
NT = S // P
HALF = S // 2
TH = NT // 2
BLOCKS = [(b, h) for b in range(NB) for h in range(2)]
REC = 2
FC = 4
NE, RANK = 8, 16
UW = P + NE
NH, HD = 16, 8
GH = 4
GW = GH * HD
NG = NH // GH
GROUPS = NB * NG
BUFS = 3
NPART = 3
STACK = NPART * NPART * HD
DEPTH = STACK + NPART
VW = 32
BIASW = 512
LAST = 510
LN_EPS, RMS_EPS = 1e-5, 1e-6
SCALE = float(P) ** -0.5
UNDERFLOW = -87.336544
N_CONSTS = 5 + NE
ONE_PAIR = float(np.array([0x3F803F80], np.uint32).view(np.float32)[0])

N_REC, N_MLP, N_FFN0, N_ATTN, N_OUT, N_FFN1 = range(6)
NORMS = [(n, b) for n in range(4) for b in range(NB)] + [(n, b) for b in range(NB) for n in (N_OUT, N_FFN1)]
NORM_AT = {nb: i for i, nb in enumerate(NORMS)}
FLIPPED_AT = {nb: i for i, nb in enumerate(x for x in NORMS if x[0] != N_OUT)}


ROW1_AFTER = (0, 1)
QK_BESIDE = 3


def logits_jobs(f, b):
    return [(f"T{f}.{b}.{h}", "act") for h in range(2)] + [(f"U{f}.{b}.{j}", "dve") for j in range(4)]


def ffn_order(f):
    jobs = []
    for q in range(len(BLOCKS) + 1):
        if q < 4:
            b, h = BLOCKS[q]
            jobs += [(f"X{f}.{b}.{h}.{k}", "act") for k in range(2)]
            jobs += [(f"HA{f}.{b}.{h}.{c}", "act") for c in range(FC)]
        if f == 0 and q == QK_BESIDE:
            jobs += q_and_k(0)
        if q >= 1:
            jobs.append(("O%d.%d.%d" % (f, *BLOCKS[q - 1]), "act"))
        if q < 4:
            jobs += [(f"HB{f}.{b}.{h}.{c}", "dve") for c in range(FC)]
        if q >= 1:
            jobs.append(("R%d.%d.%d" % (f, *BLOCKS[q - 1]), "dve"))
        if q == ROW1_AFTER[f]:
            jobs += logits_jobs(f, 1)
    return jobs


def q_and_k(b):
    return [(f"Tatt.{b}.{h}", "act") for h in range(2)] + [(f"QK.{b}.{w}.{h}", "dve") for w in range(2) for h in range(2)]


def values(b):
    return [(f"V.{b}.{h}", "dve") for h in range(2)] + [(f"CS.{b}", "dve")]


MIXER_PLAN = (("rec", 0), ("rec", 1), ("rec_out", 0), ("turn", 0), ("up", 0), ("up", 1), ("rec_out", 1), ("down", 0),
              ("down", 1), ("add", 0), ("turn", 1), ("up", 2), ("add", 1), ("down", 2), ("up", 3), ("logits", 0),
              ("add", 2), ("down", 3), ("add", 3))


def stage_jobs(stage, n):
    if stage == "rec":
        jobs = [(f"Trec.{n}.{h}", "act") for h in range(2)]
        for kind in ("XI", "A", "G"):
            for x, y in ((0, 0), (0, 1), (1, 0), (1, 1)):
                h, c = (y, x) if kind == "A" else (x, y)
                jobs.append((f"{kind}.{n}.{h}.{c}", "act"))
        return jobs
    if stage == "rec_out":
        return [(f"WO.{n}.{h}", "act") for h in range(2)] + [(f"Rrec.{n}.{h}", "dve") for h in range(2)]
    if stage == "turn":
        return [(f"Tmlp.{n}.{h}", "act") for h in range(2)]
    if stage == "logits":
        return logits_jobs(0, n)
    b, h = BLOCKS[n]
    if stage == "up":
        return [(f"{kind}.{b}.{h}.{c}", "dve") for c in range(FC) for kind in ("MG", "MU")]
    return [(f"MD.{b}.{h}", "act") if stage == "down" else (f"Rmlp.{b}.{h}", "dve")]


def dense_order():
    jobs = [job for stage, n in MIXER_PLAN for job in stage_jobs(stage, n)]
    return jobs + ffn_order(0) + values(0) + q_and_k(1) + values(1) + logits_jobs(1, 0) + ffn_order(1)


def assign_banks(order):
    bank, held, turn, turns = {}, set(), 0, list(range(8))
    for name, _ in order:
        if name == FIRST_BESIDE_RING:
            turn, turns = 0, [4, 5, 6, 7]
        if name in IN_LAST_GROUP:
            bank[name] = IN_LAST_GROUP[name]
            turn, turns = 0, [0, 1, 4, 5, 6, 7, 2, 3]
        elif name.startswith("HB"):
            bank[name] = bank["HA" + name[2:]]
            held.discard(bank[name])
        else:
            while turns[turn % len(turns)] in held:
                turn += 1
            bank[name] = turns[turn % len(turns)]
            turn += 1
            if name.startswith("HA"):
                held.add(bank[name])
    return bank


FIRST_BESIDE_RING = "Tatt.1.0"
IN_LAST_GROUP = {"T1.0.0": 0, "T1.0.1": 1, "U1.0.0": 2, "U1.0.1": 3, "U1.0.2": 0, "U1.0.3": 1}
JOBS = dense_order()
BANK = assign_banks(JOBS)
INDEX = {name: i for i, (name, _) in enumerate(JOBS)}
LAST_IN_RING = [[n for n, _ in JOBS[:INDEX[FIRST_BESIDE_RING]] if BANK[n] == k][-1] for k in range(4)]
EMPTYING = {name: (c, sum(x[1] == c for x in JOBS[: i + 1])) for i, (name, c) in enumerate(JOBS)}
BEFORE = {name: ([None] + [n for n, _ in JOBS[:i] if BANK[n] == BANK[name]])[-1] for i, (name, _) in enumerate(JOBS)}

STEPS = 2 * NT
MAXES = GH * NT
FIRST = 2
EARLY = 10
NEXT_MAXES = [("max", 1, k) for k in range(EARLY, MAXES)]
AFTER_NEXT = [("max", 2, 0), ("turn", 1, 0)] + [("max", 2, k) for k in range(1, EARLY)]
RING = NEXT_MAXES[:4] + [("bias", 0, 0), NEXT_MAXES[4], ("bias_turn", 0, 0)] + NEXT_MAXES[5:] + AFTER_NEXT + [("out", 0, 0)]
RING_AHEAD = [("max", 1, k) for k in range(MAXES)] + AFTER_NEXT
BESIDE_FIRST = EARLY - 4
TURN_BEFORE, QK_BEFORE, V_BEFORE, CS_BEFORE = 10, (12, 13, 14, 15), (18, 20), 23
BIAS_AT = RING.index(("bias", 0, 0))
RING_BEFORE_LAST = [item for item in RING if item[1] < 2]
RING_LAST = [item for item in RING if item[1] < 1]


LOGITS_STEP, ROUTE_STEP = 5, 7


def ring_of(left):
    return (RING_LAST, RING_BEFORE_LAST, RING)[min(left, 2)]


def ring_needs(items, k):
    kind, d, _ = items[k]
    made_from = {"turn": ("max", d, MAXES - 1), "bias_turn": ("bias", d, 0)}.get(kind)
    return max(k - 1, items.index(made_from) + 1) if made_from in items else k - 1


def build(nc, x_in, out, w, tab):
    ctx = ExitStack()
    with ctx:
        def sb(name, shape, dt=FP32):
            return ctx.enter_context(nc.sbuf_tensor(name, shape, dt))

        def sem(name):
            return ctx.enter_context(nc.semaphore(name))

        w_inT = sb("w_inT", [P, REC * P])
        w_gateT = sb("w_gateT", [P, REC * P])
        w_aT = sb("w_aT", [P, REC, REC * P])
        w_outT = sb("w_outT", [P, REC, P])
        mgT = sb("mgT", [P, FC * P])
        muT = sb("muT", [P, FC * P])
        mdT = sb("mdT", [P, FC, P])
        a_param = sb("a_param", [P, REC])
        ln1_w = sb("ln1_w", [P, 1])
        ln2_w = sb("ln2_w", [P, 1])
        wiT = sb("wiT", [P, FC * P])
        bi = sb("bi", [P, FC])
        woT = sb("woT", [P, FC, P])
        bo = sb("bo", [P, 1])
        bo2 = sb("bo2", [P, 1])
        agT = sb("agT", [P, UW])
        bT = sb("bT", [P, FC * P])
        gate_b = sb("gate_b", [P, NE])
        wqkvT = sb("wqkvT", [P, 3, P])
        gamma = sb("gamma", [P, P])
        beta = sb("beta", [P, P])
        t_last = sb("t_last", [P, GROUPS * GH])
        ident = sb("ident", [P, P])
        ones = sb("ones", [P, P])
        rank_of = sb("rank_of", [P, NE])
        one_pair = sb("one_pair", [P, 1])
        neghalf = sb("neghalf", [P, 2 * TH])
        tiny = sb("tiny", [P, 1])
        zero_t = sb("zero_t", [P, NT])

        x0 = sb("x0", [P, NB, NT, P])
        x = sb("x", [P, NB, NT, P])
        z = sb("z", [P, NB, NT, P])
        x1 = sb("x1", [P, NB, NT, P])
        nt = sb("nt", [P, NB, NT, P])
        v_all = x1[:].rearrange("p b t c -> p (b t c)").rearrange("p (g t c) -> p g t c", g=GROUPS, t=NT)
        o_tok = z[:].rearrange("p b t c -> p (b t c)").rearrange("p (g t c) -> p g t c", g=GROUPS, t=NT)
        stats = sb("stats", [P, NB, NT, 6])
        mv = sb("mv", [P, NB, NT, 2])
        veps = sb("veps", [P, NB, 2, 2 * TH])
        rstd = sb("rstd", [P, NB, 2, 2 * TH])
        msq = sb("msq", [P, NB, NT])
        hT = sb("hT", [P, NB, S])
        oT = sb("oT", [P, NB, S])

        DENSE = 11 * S
        TAIL = 8 * S
        arena = sb("arena", [P, NB * DENSE + TAIL])

        def carve(start, *shapes):
            tiles_ = []
            for shape in shapes:
                size = 1
                for n in shape:
                    size *= n
                flat = arena[:, start:start + size]
                axes = " ".join(f"a{i}" for i in range(len(shape)))
                tiles_.append(flat.rearrange(f"p ({axes}) -> p {axes}", **{f"a{i}": n for i, n in enumerate(shape)}) if len(shape) > 1 else flat)
                start += size
            return tiles_

        rec, mlp, moe = [], [], []
        for b in range(NB):
            rec.append(carve(b * DENSE, *[[REC, S]] * 5))
            mlp.append(carve(b * DENSE, [2, HALF], [2, HALF], [FC, S]))
            um, *others, umT = carve(b * DENSE, [2, NT, P], [FC, HALF], [2, HALF], [FC, S], [2, S])
            moe.append([*others, um, umT])
        remains, part_words = [2, S], [2 * NPART * S // 2]
        q_words, rest_0, words_0 = carve(0, [BUFS * GH * S // 2], remains, part_words)
        rest_1, words_1, pvT, biasT, vpg = carve(DENSE, remains, part_words, [S], [BIASW], [BUFS, NT, GH, VW])
        qk_rest = (rest_0, rest_1)
        qk_part = [m.bitcast(BF16).rearrange("p (w n t) -> p w n t", w=2, n=NPART) for m in (words_0, words_1)]
        probs = [m.rearrange("p w t -> p (w t)").rearrange("p (h t) -> p h t", h=GH) for m in qk_rest]
        varying = words_1[:, 0:GH * BIASW].rearrange("p (h c) -> p h c", h=GH)
        qs = q_words.bitcast(BF16).rearrange("p (n h t) -> p n h t", n=BUFS, h=GH)
        k_words, bias_raw = carve(NB * DENSE, [BUFS * GH * S // 2], [GH, BIASW])
        ks = k_words.bitcast(BF16).rearrange("p (n h t) -> p n h t", n=BUFS, h=GH)
        lg, ls, ls2, ex, key, pick0, pick1, pickd = (sb(n, [P, NB, NT, NE]) for n in
                                                     ("lg", "ls", "ls2", "ex", "key", "pick0", "pick1", "pickd"))
        m1, m2, k1, k2, esum, ersum, e2, val = (sb(n, [P, NB, NT]) for n in ("m1", "m2", "k1", "k2", "esum", "ersum", "e2", "val"))
        cs = sb("cs", [P, NB, P])
        negmax = sb("negmax", [P, BUFS, GH * NT])
        nm_rest = sb("nm_rest", [GH * NT, P])
        nm_part = sb("nm_part", [GH * NT, NPART, P], BF16)
        rl = sb("rl", [P, NT, GH])
        bias_tok = sb("bias_tok", [P, TH, GH, HD])
        pause = sb("pause", [P, 2 * TH])

        scratch = nc.dram_tensor("qk_scratch", (2, NPART, NB * P, S), BF16, kind="Internal").ap()
        banks = ctx.enter_context(nc.psum_tensor("banks", [P, 8, HALF], FP32))

        def slot_of(n):
            return banks[:, 2 * (n % 2):2 * (n % 2) + 2, :]

        def score_bank(g, n):
            return banks[:, 4 + (g * STEPS * GH + n) % 3, :]

        pv_bank = banks[:, 7, :]

        w_small = sem("w_small")
        w_rec, w_mlp, w_ffn, w_att, bo2_ready, k_ones = (sem(n) for n in ("w_rec", "w_mlp", "w_ffn", "w_att", "bo2_ready", "k_ones"))
        zeroed, consts, v_ones = sem("zeroed"), sem("consts"), sem("v_ones")
        x_loaded = [sem(f"x_loaded{b}") for b in range(NB)]
        z_ready, stored = sem("z_ready"), sem("stored")
        filled, act_emptied, dve_emptied = sem("filled"), sem("act_emptied"), sem("dve_emptied")
        stats_ready, rstd_ready, norm_ready = sem("stats_ready"), sem("rstd_ready"), sem("norm_ready")
        x1_ready, x_summed, square_ready = sem("x1_ready"), sem("x_summed"), sem("square_ready")
        x_beta = sem("x_beta")
        one_minus_sq, root_ready, y_ready, gate_sig = sem("one_minus_sq"), sem("root_ready"), sem("y_ready"), sem("gate_sig")
        logits_ready, exps_ready, second_ready, exp2_ready = (sem(n) for n in ("logits_ready", "exps_ready", "second_ready", "exp2_ready"))
        h_ready = sem("h_ready")
        qk_high, qk_mid, qk_low = sem("qk_high"), sem("qk_mid"), sem("qk_low")
        qk_stored = [sem(f"qk_stored{b}") for b in range(NB)]
        products_loaded = [[sem(f"products_loaded{n}{h}") for h in range(GH)] for n in range(BUFS)]
        bias_loaded, varying_ready, v_ready = sem("bias_loaded"), sem("varying_ready"), sem("v_ready")
        ring_filled, ring_emptied, negmax_split = sem("ring_filled"), sem("ring_emptied"), sem("negmax_split")
        negmax_loaded = sem("negmax_loaded")
        scores_filled, exp_done, pv_done, pv_out = sem("scores_filled"), sem("exp_done"), sem("pv_done"), sem("pv_out")
        PER_GROUP = {ring_filled: len(RING), ring_emptied: len(RING), negmax_split: 1, scores_filled: STEPS * GH,
                     exp_done: STEPS * GH, pv_done: STEPS, pv_out: 2, varying_ready: 1, v_ready: 1, negmax_loaded: 16 * NPART,
                     bias_loaded: 16}
        AHEAD = {ring_filled: len(RING_AHEAD), ring_emptied: len(RING_AHEAD)}
        RING_SHORT = len(RING) - len(RING_BEFORE_LAST)

        def at(G, s, k):
            short = RING_SHORT if s in (ring_filled, ring_emptied) and isinstance(G, int) and G == GROUPS - 1 else 0
            return G * PER_GROUP[s] + k + AHEAD.get(s, 0) - short

        def ring_slot(k):
            return slot_of(len(RING_AHEAD) + k)

        def emptied(name):
            engine, k = EMPTYING[name]
            return (act_emptied if engine == "act" else dve_emptied), k

        block = ctx.enter_context(nc.Block())

        def x_tiles(dram, b):
            return dram[b].rearrange("(t p) d -> p t d", p=P)

        def rows_of(m):
            return m.rearrange("(k p) n -> p k n", p=P)

        @block.sync
        def _(sp):
            sp.dma_start(x0[:, 0], x_tiles(x_in, 0)).then_inc(x_loaded[0], 16)
            for dst, src in ((w_inT[:], w["w_inT"]), (w_gateT[:], w["w_gateT"]), (w_aT[:], rows_of(w["w_aT"])),
                             (w_outT[:], rows_of(w["w_outT"]))):
                sp.dma_start(dst, src).then_inc(w_rec, 16)
            for dst, src in ((mgT[:], w["mgT"]), (muT[:], w["muT"]), (mdT[:], rows_of(w["mdT"]))):
                sp.dma_start(dst, src).then_inc(w_mlp, 16)
            for dst, src in ((agT[:], w["agT"]), (gate_b[:], w["gate_b"].broadcast_to([P, NE])), (wiT[:], w["wiT"]),
                             (bT[:], w["bT"]), (woT[:], rows_of(w["woT"]))):
                sp.dma_start(dst, src).then_inc(w_ffn, 16)
            for dst, src in ((wqkvT[:], rows_of(w["wqkvT"])), (gamma[:], w["gamma"].broadcast_to([P, P])),
                             (beta[:], w["beta"].broadcast_to([P, P])), (t_last[:], w["t_last"].broadcast_to([P, GROUPS * GH]))):
                sp.dma_start(dst, src).then_inc(w_att, 16)

            def store_parts(b):
                for k in range(4):
                    which, h = k // 2, k % 2
                    sp.wait_ge(qk_low, 4 * b + k + 1)
                    sp.dma_start(scratch[which, :, b * P:(b + 1) * P, h * HALF:(h + 1) * HALF].rearrange("n p t -> p n t"),
                                 qk_part[b][:, which, :, h * HALF:(h + 1) * HALF]).then_inc(qk_stored[b], 16)
                sp.wait_ge(qk_stored[b], 64)

            def load_products(G, buf):
                for h in range(GH):
                    head = bass.ds(G * GW + h * HD, HD)
                    for i in range(NPART):
                        rows = slice(i * NPART * HD, (i + 1) * NPART * HD)
                        sp.dma_start(qs[rows, buf, h, :], scratch[0, i, head, :].unsqueeze(0).broadcast_to([NPART, HD, S])).then_inc(products_loaded[buf][h], 16)
                        sp.dma_start(ks[rows, buf, h, :], scratch[1, :, head, :]).then_inc(products_loaded[buf][h], 16)

            def load_negmax(G, buf):
                sp.wait_ge(negmax_split, at(G, negmax_split, 1))
                for i in range(NPART):
                    sp.dma_start(qs[STACK + i:STACK + i + 1, buf, :, :].rearrange("o h (t q) -> o (h t) q", q=P),
                                 nm_part[:, i, :]).then_inc(negmax_loaded, 16)

            def load_bias(G):
                sp.dma_start(bias_raw, bass.AP(tensor=tab.tensor, offset=G * (GH * tab.shape[1]),
                                               ap=[[1, P], [tab.shape[1], GH], [1, BIASW]])).then_inc(bias_loaded, 16)

            def round_(G, n, left):
                if left >= 2:
                    sp.wait_ge(scores_filled, at(G, scores_filled, FIRST * GH))
                    load_products(G + 2, (n + 2) % BUFS)
                    sp.wait_ge(varying_ready, at(G, varying_ready, 2))
                    load_bias(G + 2)
                if left >= 1:
                    load_negmax(G + 1, (n + 1) % BUFS)

            load_bias(0)
            sp.wait_ge(k_ones, 1)
            store_parts(0)
            load_products(0, 0)
            load_products(1, 1)
            store_parts(1)
            sp.wait_ge(varying_ready, 1)
            load_bias(1)
            load_negmax(0, 0)
            with sp.Fori(0, (GROUPS - 2) // BUFS) as i:
                for n in range(BUFS):
                    round_(i * BUFS + n, n, 2)
            for G in range(GROUPS - 2, GROUPS):
                round_(G, G % BUFS, GROUPS - 1 - G)
            for b, h in BLOCKS:
                sp.wait_ge(*emptied(f"R1.{b}.{h}"))
                sp.dma_start(x_tiles(out, b)[:, h * TH:(h + 1) * TH, :], x[:, b, h * TH:(h + 1) * TH, :]).then_inc(stored, 16)
            sp.wait_ge(stored, len(BLOCKS) * 16)

        @block.gpsimd
        def _(pool):
            pool.dma_start(x0[:, 1], x_tiles(x_in, 1)).then_inc(x_loaded[1], 16)
            pool.memset(ident[:], 0.0).then_inc(zeroed, 1)
            pool.memset(neghalf[:], -0.5).then_inc(consts, 1)
            pool.memset(ones[:], 1.0).then_inc(consts, 1)
            pool.memset(tiny[:], 1e-8).then_inc(consts, 1)
            pool.memset(one_pair[:], ONE_PAIR).then_inc(consts, 1)
            for e in range(NE):
                pool.memset(rank_of[:, e:e + 1], float(NE - e)).then_inc(consts, 1)
            pool.wait_ge(zeroed, 1)
            pool.affine_select(out=ident[:], in_=ident[:], compare_op=ALU.not_equal, fill=1.0, base=0,
                               pattern=[[-1, P]], channel_multiplier=1).then_inc(consts, 1)
            pool.wait_ge(consts, N_CONSTS)

            def rstds(n, b):
                for h in range(2):
                    pool.wait_ge(stats_ready, 2 * NORM_AT[n, b] + h + 1)
                    width = 2 * TH if n == N_REC else TH
                    pool.tensor_tensor(rstd[:, b, h, 0:width], veps[:, b, h, 0:width], neghalf[:, 0:width], ALU.pow).then_inc(rstd_ready, 1)

            for b in range(NB):
                rstds(N_REC, b)
            for b in range(NB):
                pool.wait_ge(rstd_ready, 2 * NORM_AT[N_REC, b] + 2)
                for t in range(NT):
                    last = pool.tensor_scalar(z[:, b, t, :], x0[:, b, t, :], mv[:, b, t, 0:1], rstd[:, b, t // TH, t % TH:t % TH + 1],
                                              ALU.subtract, ALU.mult)
                last.then_inc(z_ready, 1)
            for b in range(NB):
                rstds(N_MLP, b)
                pool.wait_ge(x1_ready, b + 1)
                pool.tensor_tensor(x[:, b], x0[:, b], x1[:, b], ALU.add).then_inc(x_summed, 1)
            for n in (N_FFN0, N_ATTN):
                for b in range(NB):
                    rstds(n, b)

            def v_copy(G, buf):
                pool.tensor_copy(vpg[:, buf, :, :, 0:HD], v_all[:, bass.ds(G, 1), :, :].rearrange("p o t (h d) -> p (o t) h d", d=HD)).then_inc(v_ready, 1)

            pool.wait_ge(w_att, 16 * 4)
            for h in range(2):
                pool.wait_ge(rstd_ready, 2 * NORM_AT[N_ATTN, 1] + h + 1)
                for t in range(h * TH, (h + 1) * TH):
                    last = pool.tensor_scalar(nt[:, 1, t, :], x[:, 1, t, :], mv[:, 1, t, 0:1], rstd[:, 1, h, t % TH:t % TH + 1],
                                              ALU.subtract, ALU.mult)
                last.then_inc(norm_ready, 1)
            for k in range(4):
                which, h = k // 2, k % 2
                pool.wait_ge(qk_mid, 4 + k + 1)
                pool.tensor_tensor(qk_part[1][:, which, 2, h * HALF:(h + 1) * HALF], qk_rest[1][:, which, h * HALF:(h + 1) * HALF],
                                   qk_part[1][:, which, 1, h * HALF:(h + 1) * HALF], ALU.subtract).then_inc(qk_low, 1)
            for b in range(NB):
                pool.wait_ge(norm_ready, 2 * FLIPPED_AT[N_ATTN, b] + 2)
                pool.tensor_tensor(x[:, b], x[:, b], beta[:].unsqueeze(1).broadcast_to([P, NT, P]), ALU.add).then_inc(x_beta, 1)
            pool.wait_ge(*emptied("R0.1.1"))
            pool.memset(vpg, 0.0).then_inc(zeroed, 1)
            pool.wait_ge(zeroed, 2)
            pool.memset(vpg[:, :, :, :, HD:HD + 1], 1.0).then_inc(v_ones, 1)
            pool.wait_ge(v_ones, 1)

            def vary(G):
                pool.tensor_tensor(varying, bias_raw[:, :, ::-1], t_last[:, bass.ds(G * GH, GH)].unsqueeze(2).broadcast_to([P, GH, BIASW]),
                                   ALU.subtract).then_inc(varying_ready, 1)

            pool.wait_ge(*emptied("V.1.1"))
            v_copy(0, 0)
            v_copy(1, 1)
            for b in range(NB):
                pool.wait_ge(qk_stored[b], 64)
            pool.wait_ge(bias_loaded, 16)
            vary(0)

            def round_(G, n, left):
                pool.wait_ge(ring_filled, at(G, ring_filled, BIAS_AT + 1))
                pool.wait_ge(bias_loaded, at(G, bias_loaded, 32))
                pool.tensor_tensor(pause[:], neghalf[:], neghalf[:], ALU.add)
                vary(G + 1)
                if left >= 2:
                    v_copy(G + 2, (n + 2) % BUFS)
                pool.drain()

            with pool.Fori(0, (GROUPS - 2) // BUFS) as i:
                for n in range(BUFS):
                    round_(i * BUFS + n, n, 2)
            round_(GROUPS - 2, (GROUPS - 2) % BUFS, 1)
            for b in range(NB):
                rstds(N_OUT, b)
                rstds(N_FFN1, b)

        @block.scalar
        def _(act):
            for dst, src in ((ln1_w[:], w["ln1_w"]), (a_param[:], w["a_param"]), (ln2_w[:], w["ln2_w"]), (bi[:], w["bi"]), (bo[:], w["bo"])):
                act.dma_start(dst, src).then_inc(w_small, 16)

            def take(name, dst, func=ACT.Identity, signal=None, **kw):
                act.wait_ge(filled, INDEX[name] + 1)
                act.activation(dst, banks[:, BANK[name], :], func, **kw).then_inc(signal or act_emptied, 1)

            def half(tile, h):
                return tile[:, h * HALF:(h + 1) * HALF]

            def ffn(f):
                for q in range(len(BLOCKS) + 1):
                    if q < 4:
                        expand(f, q)
                    if f == 0 and q == QK_BESIDE:
                        q_and_k(0)
                    if q >= 1:
                        b, h = BLOCKS[q - 1]
                        take(f"O{f}.{b}.{h}", half(oT[:, b], h), bias=bo2[:])
                    if q == ROW1_AFTER[f]:
                        turn_norm(f, 1)
                        route(f, 1)

            def turn_norm(f, b):
                for h in range(2):
                    take(f"T{f}.{b}.{h}", half(hT[:, b], h))

            def route(f, b):
                act.wait_ge(logits_ready, NB * f + b + 1)
                act.activation(ex[:, b], ls[:, b], ACT.Exp).then_inc(exps_ready, 1)
                act.wait_ge(second_ready, NB * f + b + 1)
                act.activation(e2[:, b], m2[:, b], ACT.Exp).then_inc(exp2_ready, 1)

            def expand(f, q):
                b, h = BLOCKS[q]
                h0, _, _, _, umT = moe[b]
                for k in range(2):
                    take(f"X{f}.{b}.{h}.{k}", half(umT[:, k, :], h))
                for c in range(FC):
                    if h:
                        act.wait_ge(h_ready, (f * len(BLOCKS) + q - 1) * FC + c + 1)
                    take(f"HA{f}.{b}.{h}.{c}", h0[:, c, :], ACT.Relu, bias=bi[:, c:c + 1])

            def part_of(b, k, i):
                return half(qk_part[b][:, k // 2, i, :], k % 2)

            def mid(b, k):
                act.wait_ge(*emptied(f"QK.{b}.{k // 2}.{k % 2}"))
                act.activation(part_of(b, k, 1), half(qk_rest[b][:, k // 2, :], k % 2), ACT.Copy).then_inc(qk_mid, 1)

            def q_and_k(b):
                for h in range(2):
                    take(f"Tatt.{b}.{h}", half(hT[:, b], h))
                for k in range(4):
                    take(f"QK.{b}.{k // 2}.{k % 2}", part_of(b, k, 0), ACT.Copy, signal=qk_high)
                    if k:
                        mid(b, k - 1)
                mid(b, 3)

            act.wait_ge(consts, N_CONSTS)
            act.wait_ge(w_small, 16 * 5)

            def recurrent(b):
                xinT, gT, aT, sT, _ = rec[b]
                for h in range(2):
                    take(f"Trec.{b}.{h}", half(hT[:, b], h), scale=ln1_w[:])
                for h in range(2):
                    for c in range(REC):
                        take(f"XI.{b}.{h}.{c}", half(xinT[:, c, :], h))
                for c in range(REC):
                    for h in range(2):
                        take(f"A.{b}.{h}.{c}", half(aT[:, c, :], h), ACT.Sigmoid, bias=a_param[:, c:c + 1])
                for c in range(REC):
                    act.wait_ge(*emptied(f"A.{b}.1.{c}"))
                    act.activation(sT[:, c, :], aT[:, c, :], ACT.Square).then_inc(square_ready, 1)
                for h in range(2):
                    for c in range(REC):
                        take(f"G.{b}.{h}.{c}", half(gT[:, c, :], h), ACT.Sigmoid)
                for c in range(REC):
                    act.wait_ge(one_minus_sq, REC * b + c + 1)
                    act.activation(sT[:, c, :], sT[:, c, :], ACT.Sqrt, bias=tiny[:]).then_inc(root_ready, 1)

            def gates(q):
                b, h = BLOCKS[q]
                sg = mlp[b][0]
                for c in range(FC):
                    k = h * FC + c
                    if k >= 2:
                        act.wait_ge(*emptied(f"MG.{b}.{(k - 2) // FC}.{(k - 2) % FC}"))
                    take(f"MG.{b}.{h}.{c}", sg[:, k % 2, :], ACT.Sigmoid, signal=gate_sig)

            for stage, n in MIXER_PLAN:
                if stage == "rec":
                    recurrent(n)
                elif stage == "rec_out":
                    for h in range(2):
                        take(f"WO.{n}.{h}", half(oT[:, n], h))
                elif stage == "turn":
                    for h in range(2):
                        take(f"Tmlp.{n}.{h}", half(hT[:, n], h), scale=ln2_w[:])
                elif stage == "up":
                    gates(n)
                elif stage == "down":
                    b, h = BLOCKS[n]
                    take(f"MD.{b}.{h}", half(oT[:, b], h))
                elif stage == "logits":
                    turn_norm(0, n)
            act.activation(k_words[64:96], one_pair[64:96].broadcast_to([32, BUFS * GH * S // 2]), ACT.Copy).then_inc(k_ones, 1)
            act.wait_ge(bo2_ready, 1)
            route(0, 0)
            ffn(0)

            q_and_k(1)

            def take_pv(G, q):
                act.wait_ge(pv_done, at(G, pv_done, NT * (q + 1)))
                act.activation(half(pvT, q), pv_bank, ACT.Copy).then_inc(pv_out, 1)

            def step(G, g, s):
                if s >= 2 or not (isinstance(G, int) and G == 0):
                    act.wait_ge(pv_done, at(G, pv_done, s - 1))
                for h in range(GH):
                    n = s * GH + h
                    act.wait_ge(scores_filled, at(G, scores_filled, n + 1))
                    act.activation(probs[s % 2][:, h, :], score_bank(g, n), ACT.Exp, scale=SCALE).then_inc(exp_done, 1)
                    if h == GH - 2 and s == 0 and not (isinstance(G, int) and G == 0):
                        take_pv(G - 1, 1)
                    if h == GH - 2 and s == NT:
                        act.wait_ge(ring_filled, at(G, ring_filled, 0))
                        take_pv(G, 0)

            def round_(G, n):
                for s in range(FIRST, STEPS):
                    step(G, n, s)
                for s in range(FIRST):
                    step(G + 1, n + 1, s)

            for s in range(FIRST):
                step(0, 0, s)
            with act.Fori(0, (GROUPS - 2) // BUFS) as i:
                for n in range(BUFS):
                    round_(i * BUFS + n, n)
            round_(GROUPS - 2, GROUPS - 2)
            for s in range(FIRST, STEPS):
                step(GROUPS - 1, GROUPS - 1, s)
                if s == LOGITS_STEP:
                    turn_norm(1, 0)
            take_pv(GROUPS - 1, 1)
            route(1, 0)
            ffn(1)

        @block.vector
        def _(dve):
            def bank(name, width=HALF):
                return banks[:, BANK[name], 0:width]

            def wait_filled(name):
                dve.wait_ge(filled, INDEX[name] + 1)

            def tiles(h):
                return slice(h * TH, (h + 1) * TH)

            def tile_of(src, b, t):
                if src is o_tok:
                    return o_tok[:, b * NG:(b + 1) * NG, t, :]
                return src[:, b, t, :]

            def stats_half(n, b, src, h):
                for t in range(h * TH, (h + 1) * TH):
                    dve.bn_stats(stats[:, b, t, :], tile_of(src, b, t))
                dve.drain()
                for t in range(h * TH, (h + 1) * TH):
                    dve.bn_aggr(mv[:, b, t, :], stats[:, b, t, :])
                dve.drain()
                mean, var = mv[:, b, tiles(h), 0], mv[:, b, tiles(h), 1]
                if n == N_MLP:
                    dve.tensor_tensor(msq[:, b, tiles(h)], mean, mean, ALU.mult)
                    dve.drain()
                    dve.scalar_tensor_tensor(out=veps[:, b, h, 0:TH], in0=var, scalar=RMS_EPS, in1=msq[:, b, tiles(h)],
                                             op0=ALU.add, op1=ALU.add).then_inc(stats_ready, 1)
                elif n == N_REC:
                    dve.tensor_scalar(veps[:, b, h, TH:2 * TH], var, 1.0 + RMS_EPS, RMS_EPS * LN_EPS, ALU.mult, ALU.add)
                    dve.drain()
                    dve.tensor_scalar(veps[:, b, h, 0:TH], var, LN_EPS, None, ALU.add).then_inc(stats_ready, 1)
                else:
                    dve.tensor_scalar(veps[:, b, h, 0:TH], var, LN_EPS, None, ALU.add).then_inc(stats_ready, 1)

            def normed_half(n, b, src, h):
                dve.wait_ge(rstd_ready, 2 * NORM_AT[n, b] + h + 1)
                for t in range(h * TH, (h + 1) * TH):
                    r = rstd[:, b, h, TH + t % TH:TH + t % TH + 1] if n == N_REC else rstd[:, b, h, t % TH:t % TH + 1]
                    dst = nt[:, b, t, :]
                    if n == N_MLP:
                        last = dve.tensor_scalar(dst, tile_of(src, b, t), r, None, ALU.mult)
                    else:
                        last = dve.tensor_scalar(dst, tile_of(src, b, t), mv[:, b, t, 0:1], r, ALU.subtract, ALU.mult)
                last.then_inc(norm_ready, 1)

            def norm(n, b, src):
                dve.drain()
                for h in range(2):
                    stats_half(n, b, src, h)
                for h in range(2):
                    normed_half(n, b, src, h)

            def per_tile(v):
                return v.unsqueeze(2).broadcast_to([P, NT, NE])

            ranks = rank_of[:].unsqueeze(1).broadcast_to([P, NT, NE])

            def first_of(b, scores, top, k, pick):
                dve.tensor_tensor(key[:, b], scores[:, b], top, ALU.is_equal)
                dve.drain()
                dve.tensor_tensor(key[:, b], key[:, b], ranks, ALU.mult)
                dve.drain()
                dve.tensor_reduce(k[:, b], key[:, b], axis=AXX, op=ALU.max)
                dve.drain()
                dve.tensor_tensor(pick[:, b], ranks, per_tile(k[:, b]), ALU.is_equal)
                dve.drain()

            def route(f, b):
                for j in range(NT // 2):
                    wait_filled(f"U{f}.{b}.{j}")
                    u = bank(f"U{f}.{b}.{j}", 2 * UW).rearrange("p (t c) -> p t c", c=UW)
                    dve.tensor_tensor(lg[:, b, 2 * j:2 * j + 2, :], u[:, :, P:UW], gate_b[:].unsqueeze(1).broadcast_to([P, 2, NE]), ALU.add)
                dve.drain()
                dve.tensor_reduce(m1[:, b], lg[:, b], axis=AXX, op=ALU.max)
                dve.drain()
                dve.tensor_tensor(ls[:, b], lg[:, b], per_tile(m1[:, b]), ALU.subtract)
                dve.drain()
                dve.tensor_scalar(ls[:, b], ls[:, b], UNDERFLOW, None, ALU.max).then_inc(logits_ready, 1)
                dve.drain()
                first_of(b, ls, per_tile(zero_t[:]), k1, pick0)
                dve.scalar_tensor_tensor(out=ls2[:, b].rearrange("p t e -> p (t e)"), in0=pick0[:, b].rearrange("p t e -> p (t e)"), scalar=-1e30,
                                         in1=ls[:, b].rearrange("p t e -> p (t e)"), op0=ALU.mult, op1=ALU.add)
                dve.drain()
                dve.tensor_reduce(m2[:, b], ls2[:, b], axis=AXX, op=ALU.max).then_inc(second_ready, 1)
                dve.drain()
                first_of(b, ls2, per_tile(m2[:, b]), k2, pick1)
                dve.tensor_tensor(pickd[:, b], pick1[:, b], pick0[:, b], ALU.subtract)
                dve.drain()
                um = moe[b][3]
                for j in range(NT // 2):
                    u = bank(f"U{f}.{b}.{j}", 2 * UW).rearrange("p (t c) -> p t c", c=UW)[:, :, 0:P].rearrange("p t (e r) -> p t e r", r=RANK)
                    for k, pick in enumerate((pick0, pickd)):
                        last = dve.tensor_tensor(um[:, k, 2 * j:2 * j + 2, :].rearrange("p t (e r) -> p t e r", r=RANK), u,
                                                 pick[:, b, 2 * j:2 * j + 2, :].unsqueeze(3).broadcast_to([P, 2, NE, RANK]), ALU.mult)
                    last.then_inc(dve_emptied, 1)
                dve.wait_ge(exps_ready, NB * f + b + 1)
                dve.tensor_reduce(esum[:, b], ex[:, b], axis=AXX, op=ALU.add)
                dve.drain()
                dve.reciprocal(ersum[:, b], esum[:, b])
                dve.drain()
                dve.wait_ge(exp2_ready, NB * f + b + 1)
                dve.scalar_tensor_tensor(out=val[:, b], in0=e2[:, b], scalar=1.0, in1=ersum[:, b], op0=ALU.add, op1=ALU.mult)

            def sums(f, q):
                b, h = BLOCKS[q]
                h0, h1, hs, _, _ = moe[b]
                for c in range(FC):
                    name = f"HB{f}.{b}.{h}.{c}"
                    wait_filled(name)
                    dve.tensor_scalar(h1[:, c % 2, :], bank(name), bi[:, c:c + 1], 0.0, ALU.add, ALU.max).then_inc(dve_emptied, 1)
                    dve.wait_ge(*emptied(name))
                    dve.tensor_tensor(hs[:, c, h * HALF:(h + 1) * HALF], h1[:, c % 2, :], h0[:, c, :], ALU.add).then_inc(h_ready, 1)

            def add_ffn(f, q):
                b, h = BLOCKS[q]
                name = f"R{f}.{b}.{h}"
                wait_filled(name)
                for t in range(h * TH, (h + 1) * TH):
                    last = dve.scalar_tensor_tensor(out=x[:, b, t, :], in0=bank(name)[:, (t % TH) * P:(t % TH + 1) * P], scalar=val[:, b, t:t + 1],
                                                    in1=x[:, b, t, :], op0=ALU.mult, op1=ALU.add)
                last.then_inc(dve_emptied, 1)

            def ffn(f, beside):
                for q in range(len(BLOCKS) + 1):
                    if q in beside:
                        beside[q]()
                    if q < 4:
                        sums(f, q)
                    if q >= 1:
                        add_ffn(f, q - 1)
                    if q == ROW1_AFTER[f]:
                        route(f, 1)

            dve.memset(zero_t[:], 0.0)
            for b in range(NB):
                dve.wait_ge(x_loaded[b], 16)
                norm(N_REC, b, x0)
            dve.wait_ge(w_small, 16 * 5)
            dve.tensor_scalar(bo2[:], bo[:], 2.0, None, ALU.mult).then_inc(bo2_ready, 1)

            def one_minus(b):
                sT = rec[b][3]
                for c in range(REC):
                    dve.wait_ge(square_ready, REC * b + c + 1)
                    dve.tensor_scalar(sT[:, c, :], sT[:, c, :], -1.0, 1.0, ALU.mult, ALU.add).then_inc(one_minus_sq, 1)

            def scan(b, c):
                xinT, gT, aT, sT, yT = rec[b]
                dve.wait_ge(root_ready, REC * b + c + 1)
                dve.tensor_tensor(sT[:, c, :], sT[:, c, :], xinT[:, c, :], ALU.mult)
                dve.drain()
                dve.tensor_tensor_scan(yT[:, c, :], aT[:, c, :], sT[:, c, :], 0.0, ALU.mult, ALU.add)
                dve.drain()
                dve.wait_ge(*emptied(f"G.{b}.1.{c}"))
                dve.tensor_tensor(yT[:, c, :], yT[:, c, :], gT[:, c, :], ALU.mult).then_inc(y_ready, 1)

            def add_rec(b):
                dve.wait_ge(z_ready, b + 1)
                for h in range(2):
                    wait_filled(f"Rrec.{b}.{h}")
                    dve.tensor_tensor(x1[:, b, tiles(h), :], z[:, b, tiles(h), :], bank(f"Rrec.{b}.{h}").rearrange("p (t d) -> p t d", d=P), ALU.add).then_inc(dve_emptied, 1)
                    dve.drain()
                    stats_half(N_MLP, b, x1, h)
                dve.nop().then_inc(x1_ready, 1)
                for h in range(2):
                    normed_half(N_MLP, b, x1, h)

            def products(q):
                b, h = BLOCKS[q]
                sg, sgu, m_T = mlp[b]
                for c in range(FC):
                    k = h * FC + c
                    dve.wait_ge(gate_sig, q * FC + c + 1)
                    dve.tensor_tensor(sgu[:, k % 2, :], sg[:, k % 2, :], bank(f"MG.{b}.{h}.{c}"), ALU.mult).then_inc(dve_emptied, 1)
                    wait_filled(f"MU.{b}.{h}.{c}")
                    dve.wait_ge(*emptied(f"MG.{b}.{h}.{c}"))
                    dve.tensor_tensor(m_T[:, c, h * HALF:(h + 1) * HALF], sgu[:, k % 2, :], bank(f"MU.{b}.{h}.{c}"), ALU.mult).then_inc(dve_emptied, 1)

            def add_mlp(q):
                b, h = BLOCKS[q]
                dve.wait_ge(x_summed, b + 1)
                wait_filled(f"Rmlp.{b}.{h}")
                dve.tensor_tensor(x[:, b, tiles(h), :], x[:, b, tiles(h), :], bank(f"Rmlp.{b}.{h}").rearrange("p (t d) -> p t d", d=P), ALU.add).then_inc(dve_emptied, 1)

            one_minus(0)
            for c in range(REC):
                scan(0, c)
            one_minus(1)
            add_rec(0)
            scan(1, 0)
            products(0)
            scan(1, 1)
            products(1)
            add_rec(1)
            dve.wait_ge(w_ffn, 16 * 5)
            add_mlp(0)
            products(2)
            add_mlp(1)
            norm(N_FFN0, 0, x)
            products(3)
            route(0, 0)
            add_mlp(2)
            add_mlp(3)
            norm(N_FFN0, 1, x)

            def part_of(b, k, i):
                return qk_part[b][:, k // 2, i, (k % 2) * HALF:(k % 2 + 1) * HALF]

            def rest_of(b, k):
                return qk_rest[b][:, k // 2, (k % 2) * HALF:(k % 2 + 1) * HALF]

            def low(b, k):
                dve.wait_ge(qk_mid, 4 * b + k + 1)
                dve.tensor_tensor(part_of(b, k, 2), rest_of(b, k), part_of(b, k, 1), ALU.subtract).then_inc(qk_low, 1)

            def rest(b, k):
                dve.wait_ge(qk_high, 4 * b + k + 1)
                dve.tensor_tensor(rest_of(b, k), bank(f"QK.{b}.{k // 2}.{k % 2}"), part_of(b, k, 0), ALU.subtract).then_inc(dve_emptied, 1)

            def take_values(b, h):
                wait_filled(f"V.{b}.{h}")
                dve.tensor_copy(v_all[:, b * NG:(b + 1) * NG, tiles(h), :], bank(f"V.{b}.{h}").rearrange("p (t g c) -> p g t c", g=NG, c=GW)).then_inc(dve_emptied, 1)

            def take_sum(b):
                wait_filled(f"CS.{b}")
                dve.tensor_tensor(cs[:, b].rearrange("p (h d) -> p h d", d=HD), bank(f"CS.{b}", P).rearrange("p (h d) -> p h d", d=HD),
                                  t_last[:, b * NH:(b + 1) * NH].unsqueeze(2).broadcast_to([P, NH, HD]), ALU.mult).then_inc(dve_emptied, 1)

            def row_0():
                norm(N_ATTN, 0, x)
                for k in range(4):
                    rest(0, k)
                    if k:
                        low(0, k - 1)
                low(0, 3)

            ffn(0, {QK_BESIDE: row_0})
            dve.wait_ge(w_att, 16 * 4)
            for h in range(2):
                take_values(0, h)
            take_sum(0)

            def max_item(slot, buf, k):
                return dve.tensor_reduce(negmax[:, buf, k:k + 1], slot.rearrange("p a b -> p (a b)"), axis=AXX, op=ALU.max, negate=True)

            def split_negmax(slot):
                rows = slot[0:GH * NT, 0, 0:P]
                dve.tensor_copy(nm_part[:, 0, :], rows)
                dve.drain()
                dve.tensor_tensor(nm_rest[:], rows, nm_part[:, 0, :], ALU.subtract).then_inc(ring_emptied, 1)
                dve.drain()
                dve.tensor_copy(nm_part[:, 1, :], nm_rest[:])
                dve.drain()
                dve.tensor_tensor(nm_part[:, 2, :], nm_rest[:], nm_part[:, 1, :], ALU.subtract).then_inc(negmax_split, 1)

            def constant_part(G):
                part = cs[:].rearrange("p b (g c) -> p (b g) c", g=NG)[:, bass.ds(G, 1), :]
                return part.rearrange("p o (h d) -> p o h d", d=HD).broadcast_to([P, TH, GH, HD])

            def empty(G, g, item, slot):
                kind, d, k = item
                if kind == "max":
                    max_item(slot, (g + d) % BUFS, k).then_inc(ring_emptied, 1)
                elif kind == "turn":
                    split_negmax(slot)
                elif kind == "bias":
                    dve.tensor_copy(biasT, slot[:, 0, :]).then_inc(ring_emptied, 1)
                elif kind == "bias_turn":
                    dve.tensor_tensor(bias_tok[:], slot[:, 0, :].rearrange("p (t g v) -> p t g v", g=GH, v=VW)[:, :, :, 0:HD],
                                      constant_part(G), ALU.add).then_inc(ring_emptied, 1)
                else:
                    o = slot.rearrange("p a (t g v) -> p (a t) g v", g=GH, v=VW)
                    dst = o_tok[:, bass.ds(G, 1), :, :].rearrange("p o t (g d) -> p (o t) g d", d=HD)
                    dve.reciprocal(rl[:], o[:, :, :, HD])
                    dve.drain()
                    dve.tensor_tensor(dst, o[:, :, :, 0:HD], rl[:].unsqueeze(3).broadcast_to([P, NT, GH, HD]), ALU.mult).then_inc(ring_emptied, 1)
                    dve.drain()
                    dve.tensor_tensor(dst[:, 0:TH], dst[:, 0:TH], bias_tok[:], ALU.add)
                    dve.tensor_tensor(dst[:, TH:NT], dst[:, TH:NT], constant_part(G), ALU.add)
                    dve.drain()

            def empty_ahead(start, stop):
                for k in range(start, stop):
                    dve.wait_ge(ring_filled, k + 1)
                    empty(None, -1, RING_AHEAD[k], slot_of(k))

            dve.drain()
            for h in range(2):
                stats_half(N_ATTN, 1, x, h)
            done = 0
            for k in range(4):
                empty_ahead(done, QK_BEFORE[k])
                done = QK_BEFORE[k]
                rest(1, k)
            for h in range(2):
                empty_ahead(done, V_BEFORE[h])
                done = V_BEFORE[h]
                take_values(1, h)
            empty_ahead(done, CS_BEFORE)
            take_sum(1)
            empty_ahead(CS_BEFORE, len(RING_AHEAD))

            def round_items(G, g, items, first=0):
                for k, item in enumerate(items, first):
                    dve.wait_ge(ring_filled, at(G, ring_filled, k + 1))
                    empty(G, g, item, ring_slot(k))

            def attended_out(b):
                dve.drain()
                for h in range(2):
                    stats_half(N_OUT, b, o_tok, h)
                for t in range(NT):
                    dve.scalar_tensor_tensor(out=nt[:, b, t, :].rearrange("p (g c) -> p g c", g=NG), in0=tile_of(o_tok, b, t),
                                             scalar=mv[:, b, t, 0:1], in1=gamma[:].rearrange("p (g c) -> p g c", g=NG),
                                             op0=ALU.subtract, op1=ALU.mult)

            def finish_row_1():
                attended(1)

            def attended(b):
                dve.drain()
                dve.wait_ge(x_beta, b + 1)
                for h in range(2):
                    dve.wait_ge(rstd_ready, 2 * NORM_AT[N_OUT, b] + h + 1)
                    for t in range(h * TH, (h + 1) * TH):
                        dve.scalar_tensor_tensor(out=x[:, b, t, :], in0=nt[:, b, t, :], scalar=rstd[:, b, h, t % TH:t % TH + 1],
                                                 in1=x[:, b, t, :], op0=ALU.mult, op1=ALU.add)
                norm(N_FFN1, b, x)

            with dve.Fori(0, (GROUPS - 2) // BUFS) as i:
                for n in range(BUFS):
                    round_items(i * BUFS + n, n, RING)
            round_items(GROUPS - 2, GROUPS - 2, RING_BEFORE_LAST[:-1])
            attended_out(0)
            attended(0)
            round_items(GROUPS - 2, GROUPS - 2, RING_BEFORE_LAST[-1:], len(RING_BEFORE_LAST) - 1)
            round_items(GROUPS - 1, GROUPS - 1, RING_LAST[:2])
            route(1, 0)
            round_items(GROUPS - 1, GROUPS - 1, RING_LAST[2:], 2)
            attended_out(1)
            ffn(1, {1: finish_row_1})

        @block.tensor
        def _(pe):
            def begin(name):
                if BEFORE[name]:
                    pe.wait_ge(*emptied(BEFORE[name]))

            def dense(name, terms):
                begin(name)
                for i, (lhsT, rhs) in enumerate(terms):
                    last = pe.matmul(banks[:, BANK[name], :], lhsT, rhs, start=i == 0, stop=i == len(terms) - 1)
                last.then_inc(filled, 1)

            def flip(name, blocks):
                begin(name)
                for i, src in enumerate(blocks):
                    last = pe.transpose(banks[:, BANK[name], i * P:(i + 1) * P], src, ident[:])
                last.then_inc(filled, 1)

            def half(tile, h):
                return tile[:, h * HALF:(h + 1) * HALF]

            def chunk(tile, c):
                return tile[:, c * P:(c + 1) * P]

            def flip_norm(n, b, prefix):
                for h in range(2):
                    pe.wait_ge(norm_ready, 2 * FLIPPED_AT[n, b] + h + 1)
                    flip(f"{prefix}.{b}.{h}", [nt[:, b, h * TH + i, :] for i in range(TH)])

            def back(src_job, job, b, h):
                pe.wait_ge(*emptied(f"{src_job}.{b}.{h}"))
                flip(f"{job}.{b}.{h}", [chunk(oT[:, b], h * TH + i) for i in range(TH)])

            def logits(f, b):
                for j in range(NT // 2):
                    name = f"U{f}.{b}.{j}"
                    pe.wait_ge(*emptied(f"T{f}.{b}.{j // 2}"))
                    begin(name)
                    for i in range(2):
                        last = pe.matmul(banks[:, BANK[name], i * UW:(i + 1) * UW], chunk(hT[:, b], 2 * j + i), agT[:], start=True, stop=True)
                    last.then_inc(filled, 1)

            def key_or_query(b, k):
                which, h = k // 2, k % 2
                pe.wait_ge(*emptied(f"Tatt.{b}.{h}"))
                dense(f"QK.{b}.{which}.{h}", [(wqkvT[:, which, :], half(hT[:, b], h))])

            def value_half(b, h):
                name = f"V.{b}.{h}"
                begin(name)
                for i in range(TH):
                    last = pe.matmul(banks[:, BANK[name], i * P:(i + 1) * P], chunk(hT[:, b], h * TH + i), wqkvT[:, 2, :], start=True, stop=True)
                last.then_inc(filled, 1)

            def value_sum(b):
                begin(f"CS.{b}")
                pe.wait_ge(*emptied(f"V.{b}.1"))
                for t in range(NT):
                    last = pe.matmul(banks[:, BANK[f"CS.{b}"], 0:P], ones[:], v_all[:, b * NG:(b + 1) * NG, t, :], start=t == 0, stop=t == NT - 1)
                last.then_inc(filled, 1)

            def ffn(f):

                def base(b, h, c):
                    begin(f"HA{f}.{b}.{h}.{c}")
                    pe.matmul(banks[:, BANK[f"HA{f}.{b}.{h}.{c}"], :], chunk(wiT, c), half(hT[:, b], h), start=True, stop=False, skip_group_check=True)

                def lora(name, b, h, c, k):
                    pe.matmul(banks[:, BANK[name], :], chunk(bT, c), half(moe[b][4][:, k, :], h), start=False, stop=k == 1, skip_group_check=True).then_inc(filled, 1)

                for q in range(len(BLOCKS) + 1):
                    if q < 4:
                        b, h = BLOCKS[q]
                        if h == 0:
                            pe.wait_ge(*emptied(f"U{f}.{b}.3"))
                        if f == 1 and q == 1:
                            pe.wait_ge(ring_emptied, at(GROUPS - 1, ring_emptied, len(RING_LAST)))
                        for k in range(2):
                            flip(f"X{f}.{b}.{h}.{k}", [moe[b][3][:, k, h * TH + i, :] for i in range(TH)])
                        base(b, h, 0)
                        base(b, h, 1)
                        pe.wait_ge(*emptied(f"X{f}.{b}.{h}.1"))
                        for c in range(FC):
                            if c >= 2:
                                base(b, h, c)
                            lora(f"HA{f}.{b}.{h}.{c}", b, h, c, 0)
                    if f == 0 and q == QK_BESIDE:
                        pe.wait_ge(w_att, 16 * 4)
                        flip_norm(N_ATTN, 0, "Tatt")
                        for k in range(4):
                            key_or_query(0, k)
                    if q >= 1:
                        b, h = BLOCKS[q - 1]
                        pe.wait_ge(h_ready, (f * len(BLOCKS) + q) * FC)
                        dense(f"O{f}.{b}.{h}", [(woT[:, c, :], half(moe[b][2][:, c, :], h)) for c in range(FC)])
                    if q < 4:
                        b, h = BLOCKS[q]
                        for c in range(FC):
                            pe.wait_ge(*emptied(f"HA{f}.{b}.{h}.{c}"))
                            lora(f"HB{f}.{b}.{h}.{c}", b, h, c, 1)
                    if q >= 1:
                        back(f"O{f}", f"R{f}", *BLOCKS[q - 1])
                    if q == ROW1_AFTER[f]:
                        flip_norm((N_FFN0, N_FFN1)[f], 1, f"T{f}")
                        logits(f, 1)

            pe.wait_ge(consts, N_CONSTS)

            def recurrent(b):
                xinT = rec[b][0]
                flip_norm(N_REC, b, "Trec")
                pe.wait_ge(w_rec, 16 * 4)
                for h in range(2):
                    pe.wait_ge(*emptied(f"Trec.{b}.{h}"))
                    for c in range(REC):
                        dense(f"XI.{b}.{h}.{c}", [(chunk(w_inT, c), half(hT[:, b], h))])
                for c in range(REC):
                    for h in range(2):
                        pe.wait_ge(*emptied(f"XI.{b}.{h}.1"))
                        dense(f"A.{b}.{h}.{c}", [(chunk(w_aT[:, k, :], c), half(xinT[:, k, :], h)) for k in range(REC)])
                for h in range(2):
                    for c in range(REC):
                        dense(f"G.{b}.{h}.{c}", [(chunk(w_gateT, c), half(hT[:, b], h))])

            for stage, n in MIXER_PLAN:
                if stage == "rec":
                    recurrent(n)
                elif stage == "rec_out":
                    pe.wait_ge(y_ready, REC * (n + 1))
                    for h in range(2):
                        dense(f"WO.{n}.{h}", [(w_outT[:, k, :], half(rec[n][4][:, k, :], h)) for k in range(REC)])
                    for h in range(2):
                        back("WO", "Rrec", n, h)
                elif stage == "turn":
                    flip_norm(N_MLP, n, "Tmlp")
                elif stage == "up":
                    b, h = BLOCKS[n]
                    pe.wait_ge(w_mlp, 16 * 3)
                    pe.wait_ge(*emptied(f"Tmlp.{b}.{h}"))
                    for c in range(FC):
                        dense(f"MG.{b}.{h}.{c}", [(chunk(mgT, c), half(hT[:, b], h))])
                        dense(f"MU.{b}.{h}.{c}", [(chunk(muT, c), half(hT[:, b], h))])
                elif stage == "down":
                    b, h = BLOCKS[n]
                    pe.wait_ge(*emptied(f"MU.{b}.{h}.{FC - 1}"))
                    dense(f"MD.{b}.{h}", [(mdT[:, c, :], half(mlp[b][2][:, c, :], h)) for c in range(FC)])
                elif stage == "add":
                    back("MD", "Rmlp", *BLOCKS[n])
                else:
                    pe.wait_ge(w_ffn, 16 * 5)
                    flip_norm(N_FFN0, n, "T0")
                    logits(0, n)
            ffn(0)
            for h in range(2):
                value_half(0, h)
            value_sum(0)

            def max_item(G, g, slot, d, k):
                buf = (g + d) % BUFS
                h, t = k // NT, k % NT
                if t == 0:
                    pe.wait_ge(products_loaded[buf][h], (G + d - buf) * (16 * 2 * NPART // BUFS) + 16 * 2 * NPART)
                for half_ in range(2):
                    last = pe.matmul(slot[:, half_, :], qs[0:STACK, buf, h, t * P:(t + 1) * P], ks[0:STACK, buf, h, half_ * HALF:(half_ + 1) * HALF],
                                     start=True, stop=True)
                return last

            def turn_maxes(g, slot, d):
                return pe.transpose(slot[0:GH * NT, 0, 0:P], negmax[:, (g + d) % BUFS, :], ident[:])

            def bias_part(G, g, slot):
                pe.wait_ge(varying_ready, at(G, varying_ready, 1))
                for t in range(NT - 1, TH - 1, -1):
                    skip = (NT - 1 - t) * P
                    for h in range(GH):
                        last = pe.matmul(slot[32 * h:32 * h + VW, 0, 0:BIASW - skip], vpg[:, g % BUFS, t, h, :], varying[:, h, skip:BIASW],
                                         start=t == NT - 1, stop=t == TH)
                return last

            def turn_bias(slot):
                for t in range(TH):
                    last = pe.transpose(slot[:, 0, t * P:(t + 1) * P], chunk(biasT, t), ident[:])
                return last

            def turn_out(G, slot):
                pe.wait_ge(pv_out, at(G, pv_out, 2))
                for t in range(NT):
                    last = pe.transpose(slot[:, t // TH, (t % TH) * P:(t % TH + 1) * P], chunk(pvT, t), ident[:])
                return last

            def fill(G, g, item, slot):
                kind, d, k = item
                if kind == "max":
                    last = max_item(G, g, slot, d, k)
                elif kind == "turn":
                    last = turn_maxes(g, slot, d)
                elif kind == "bias":
                    last = bias_part(G, g, slot)
                elif kind == "bias_turn":
                    last = turn_bias(slot)
                else:
                    last = turn_out(G, slot)
                last.then_inc(ring_filled, 1)

            def fill_ahead(k):
                if ring_needs(RING_AHEAD, k) > 0:
                    pe.wait_ge(ring_emptied, ring_needs(RING_AHEAD, k))
                fill(-1, -1, RING_AHEAD[k], slot_of(k))

            def fill_round(G, g, items, k):
                pe.wait_ge(ring_emptied, at(G, ring_emptied, ring_needs(items, k)))
                fill(G, g, items[k], ring_slot(k))

            def scores(G, g, s, h):
                n = s * GH + h
                if n == 0:
                    pe.wait_ge(negmax_loaded, at(G, negmax_loaded, 16 * NPART))
                if n >= 3 or not (isinstance(G, int) and G == 0):
                    pe.wait_ge(exp_done, at(G, exp_done, n - 2))
                t, q = s % NT, s // NT
                pe.matmul(score_bank(g, n), ks[0:DEPTH, g % BUFS, h, t * P:(t + 1) * P], qs[0:DEPTH, g % BUFS, h, q * HALF:(q + 1) * HALF],
                          start=True, stop=True).then_inc(scores_filled, 1)

            def weigh(G, g, s):
                t, q = s % NT, s // NT
                pe.wait_ge(exp_done, at(G, exp_done, (s + 1) * GH))
                if t == 0:
                    if q == 0:
                        pe.wait_ge(v_ready, at(G, v_ready, 1))
                    if q or not (isinstance(G, int) and G == 0):
                        pe.wait_ge(pv_out, at(G, pv_out, q))
                for h in range(GH):
                    last = pe.matmul(pv_bank[32 * h:32 * h + VW, :], vpg[:, g % BUFS, t, h, :], probs[s % 2][:, h, :],
                                     start=t == 0, stop=t == NT - 1)
                last.then_inc(pv_done, 1)

            def step(G, g, s, fill_item, ring):
                scores(G, g, s, 0)
                if len(ring) > 0:
                    fill_item(ring[0])
                scores(G, g, s, 1)
                scores(G, g, s, 2)
                if s:
                    weigh(G, g, s - 1)
                elif not (isinstance(G, int) and G == 0):
                    weigh(G - 1, g - 1, STEPS - 1)
                if len(ring) > 1:
                    fill_item(ring[1])
                scores(G, g, s, 3)
                for k in ring[2:]:
                    fill_item(k)

            def beside(items, j):
                share = RING[j * len(RING) // STEPS:(j + 1) * len(RING) // STEPS]
                return [items.index(x) for x in share if x in items]

            def round_(G, g, items):
                def fill_item(k):
                    fill_round(G, g, items, k)

                for j in range(STEPS):
                    s = FIRST + j
                    step(G + s // STEPS, g + s // STEPS, s % STEPS, fill_item, beside(items, j))

            for name in LAST_IN_RING:
                pe.wait_ge(*emptied(name))
            done = 0

            def fill_up_to(done, stop):
                for k in range(done, stop):
                    fill_ahead(k)
                return stop

            done = fill_up_to(done, TURN_BEFORE)
            flip_norm(N_ATTN, 1, "Tatt")
            for k in range(4):
                done = fill_up_to(done, QK_BEFORE[k])
                key_or_query(1, k)
            for h in range(2):
                done = fill_up_to(done, V_BEFORE[h])
                value_half(1, h)
            done = fill_up_to(done, CS_BEFORE)
            value_sum(1)
            fill_up_to(done, len(RING_AHEAD) - BESIDE_FIRST)
            pe.wait_ge(*emptied("CS.1"))
            for s in range(FIRST):
                share = BESIDE_FIRST // FIRST + s * (BESIDE_FIRST % FIRST)
                start = len(RING_AHEAD) - (BESIDE_FIRST if s == 0 else share)
                step(0, 0, s, fill_ahead, list(range(start, start + share)))
            with pe.Fori(0, (GROUPS - 2) // BUFS) as i:
                for n in range(BUFS):
                    round_(i * BUFS + n, n, RING)
            round_(GROUPS - 2, GROUPS - 2, RING_BEFORE_LAST)
            G = GROUPS - 1

            def fill_last(k):
                fill_round(G, G, RING_LAST, k)

            for j in range(STEPS - FIRST):
                s = FIRST + j
                step(G, G, s, fill_last, [j] if j < 2 else [])
                if s == LOGITS_STEP:
                    pe.wait_ge(ring_emptied, at(G, ring_emptied, 2))
                    flip_norm(N_FFN1, 0, "T1")
                if s == ROUTE_STEP:
                    logits(1, 0)
            weigh(G, G, STEPS - 1)
            pe.wait_ge(*emptied("U1.0.3"))
            fill_last(2)
            ffn(1)
    return nc


def kernel(**inputs):
    import concourse.bacc as bacc
    from concourse.bass_utils import run_bass_kernel_spmd

    a = {k[3:]: np.asarray(v) for k, v in inputs.items()}

    def col(v, n=1):
        return v.reshape(n, P).T

    clipped = np.minimum(np.arange(P - 1 + BIASW), LAST)
    laid = {
        "x": a["attn_a_x"], "ln1_w": col(a["attn_a_ln1_w"]), "ln2_w": col(a["attn_a_ln2_w"]),
        "w_inT": a["attn_a_w_in"].T, "w_gateT": a["attn_a_w_gate"].T, "w_aT": a["attn_a_w_a"].T, "w_outT": a["attn_a_w_out"].T,
        "a_param": col(a["attn_a_a_param"], REC), "mgT": a["attn_a_w_mlp_gate"].T, "muT": a["attn_a_w_mlp_up"].T,
        "mdT": a["attn_a_w_mlp_down"].T,
        "wqkvT": np.concatenate([a["attn_b_Wq"].T, a["attn_b_Wk"].T, a["attn_b_Wv"].T]),
        "tab": np.tile(a["attn_b_rel_bias_table"].T[:, clipped[::-1]], (NB, 1)),
        "t_last": np.tile(a["attn_b_rel_bias_table"][LAST:LAST + 1], (1, NB)),
        "gamma": a["attn_b_ln_gamma"].reshape(1, P), "beta": a["attn_b_ln_beta"].reshape(1, P),
        "wiT": a["ffn_wi"].T, "bi": col(a["ffn_bi"], FC), "woT": a["ffn_wo"].T, "bo": col(a["ffn_bo"]),
        "agT": np.concatenate([a["ffn_lora_A"].reshape(P, P), a["ffn_gate_w"]]).T,
        "bT": a["ffn_lora_B"].transpose(0, 2, 1).reshape(P, FC * P), "gate_b": a["ffn_gate_b"].reshape(1, NE),
    }
    nc = bacc.Bacc("TRN2", target_bir_lowering=False, num_devices=1)
    arrays, aps = {}, {}
    for name, v in laid.items():
        arrays[f"in_{name}"] = np.ascontiguousarray(v)
        aps[name] = nc.dram_tensor(f"in_{name}", v.shape, FP32, kind="ExternalInput").ap()
    out = nc.dram_tensor("out", (NB, S, P), FP32, kind="ExternalOutput").ap()
    build(nc, aps.pop("x"), out, aps, aps.pop("tab"))
    return run_bass_kernel_spmd(nc, [arrays], core_ids=[0]).results[0]["out"]
```
